# Optimizing a Trainium2 kernel written in Bass

```python
import numpy as np
import jax
import jax.numpy as jnp

def _softmax(x, axis=-1):
    return jax.nn.softmax(x, axis=axis)

def _gelu(x):
    return jax.nn.gelu(x, approximate=True)

def _silu(x):
    return jax.nn.silu(x)

def _sigmoid(x):
    return jax.nn.sigmoid(x)

def _layernorm(x, axis=-1, eps=1e-05):
    m = jnp.mean(x, axis=axis, keepdims=True)
    v = jnp.var(x, axis=axis, keepdims=True)
    return (x - m) / jnp.sqrt(v + eps)

def _scatter_add(tgt, idx, src, axis=0):
    return tgt.at[idx].add(src)

def _segment_sum(src, seg, n):
    return jax.ops.segment_sum(src, seg, n)
kernel_name = 'mk_gps_d1_gnn_r32_a7fd4b'

def setup_inputs(seed: int=0):
    np.random.seed(seed)
    _w = jnp.asarray

    def _rec_inputs():
        import jax
        import jax.numpy as jnp
        _gk = jax.random.key(seed)
        x = -8.776e-05 + 1 * jax.random.normal(jax.random.fold_in(_gk, 1), (10000, 512), jnp.float32)
        src = jax.random.randint(jax.random.fold_in(_gk, 2), (10000,), 0, 10000, jnp.int32)
        dst = jax.random.randint(jax.random.fold_in(_gk, 3), (10000,), 0, 10000, jnp.int32)
        _o = jnp.argsort(dst, stable=True)
        src = src[_o]
        dst = dst[_o]
        return (x, src, dst)
    x, src, dst = _rec_inputs()

    def _L0_gnn_setup():
        import jax, jax.numpy as jnp
        import numpy as np
        N_NODES = 10000
        N_EDGES = 5000
        D_IN = 512
        D_HID = 512
        D_OUT = 512

        def _sage_conv(x, src, dst, W_l, W_r, b):
            n = x.shape[0]
            summed = jax.ops.segment_sum(x[src], dst, num_segments=n)
            deg = jax.ops.segment_sum(jnp.ones((src.shape[0],), x.dtype), dst, num_segments=n)
            agg = summed / jnp.maximum(deg, 1.0)[:, None]
            return agg @ W_l.T + x @ W_r.T + b
        key = jax.random.key(seed)
        ks = jax.random.split(key, 8)
        x = jax.random.normal(ks[0], (N_NODES, D_IN), dtype=jnp.float32)
        edge_index = jax.random.randint(ks[1], (2, N_EDGES), 0, N_NODES, dtype=jnp.int64)
        label = jax.random.randint(ks[2], (1,), 0, 3, dtype=jnp.int64)
        batch = jnp.zeros((N_NODES,), dtype=jnp.int64)
        s1 = 1.0 / np.sqrt(D_IN)
        s2 = 1.0 / np.sqrt(D_HID)
        W1_l = jax.random.normal(ks[3], (D_HID, D_IN), dtype=jnp.float32) * s1
        W1_r = jax.random.normal(ks[4], (D_HID, D_IN), dtype=jnp.float32) * s1
        b1 = jnp.zeros((D_HID,), dtype=jnp.float32)
        W2_l = jax.random.normal(ks[5], (D_OUT, D_HID), dtype=jnp.float32) * s2
        W2_r = jax.random.normal(ks[6], (D_OUT, D_HID), dtype=jnp.float32) * s2
        b2 = jnp.zeros((D_OUT,), dtype=jnp.float32)
        return {'x': x, 'label': label, 'edge_index': edge_index, 'batch': batch, 'W1_l': W1_l, 'W1_r': W1_r, 'b1': b1, 'W2_l': W2_l, 'W2_r': W2_r, 'b2': b2}
    _L0_gnn_all = _L0_gnn_setup()
    _L0_gnn_in = {k: v for k, v in _L0_gnn_all.items() if k in ('label', 'W1_l', 'W1_r', 'b1', 'W2_l', 'W2_r', 'b2')}
    del _L0_gnn_all

    def _L0_mix_setup():
        import jax, jax.numpy as jnp
        import numpy as np
        DIM, HEADS, NB_FEATURES = (512, 8, 64)
        HEAD_DIM = DIM // HEADS

        def _phi(t, proj_mat):
            return jax.nn.elu(jnp.einsum('bnhd,hdf->bnhf', t, proj_mat)) + 1.0
        key = jax.random.key(seed)
        k_x, k_qkv, k_pm, k_wp, k_bp = jax.random.split(key, 5)
        B, N = (8, 128)
        x = jax.random.normal(k_x, (B, N, DIM), dtype=jnp.float32)
        w_qkv = jax.random.normal(k_qkv, (DIM, 3 * DIM), dtype=jnp.float32) * (1.0 / np.sqrt(DIM))
        proj_mat = jax.random.normal(k_pm, (HEADS, HEAD_DIM, NB_FEATURES), dtype=jnp.float32)
        w_proj = jax.random.normal(k_wp, (DIM, DIM), dtype=jnp.float32) * (1.0 / np.sqrt(DIM))
        b_proj = jax.random.normal(k_bp, (DIM,), dtype=jnp.float32) * 0.01
        return {'x': x, 'w_qkv': w_qkv, 'proj_mat': proj_mat, 'w_proj': w_proj, 'b_proj': b_proj}
    _L0_mix_all = _L0_mix_setup()
    _L0_mix_in = {k: v for k, v in _L0_mix_all.items() if k in ('w_qkv', 'proj_mat', 'w_proj', 'b_proj')}
    del _L0_mix_all

    def _L0_ffn_setup():
        import jax, jax.numpy as jnp
        import numpy as np
        B, S, D = (8, 128, 512)
        H = 64
        O = 512
        E = 8
        TOP_K = 1
        key = jax.random.key(seed)
        ks = jax.random.split(key, 8)
        sc = 0.02
        return {'x': jax.random.normal(ks[0], (B, S, D), dtype=jnp.float32), 'Wr': jax.random.normal(ks[1], (D, E), dtype=jnp.float32) * sc, 'br': jnp.zeros((E,), dtype=jnp.float32), 'W1': jax.random.normal(ks[2], (E, D, H), dtype=jnp.float32) * sc, 'b1': jnp.zeros((E, H), dtype=jnp.float32), 'W2': jax.random.normal(ks[3], (E, H, O), dtype=jnp.float32) * sc, 'b2': jnp.zeros((E, O), dtype=jnp.float32)}
    _L0_ffn_all = _L0_ffn_setup()
    _L0_ffn_in = {k: v for k, v in _L0_ffn_all.items() if k in ('Wr', 'br', 'W1', 'b1', 'W2', 'b2')}
    del _L0_ffn_all
    return {'x': x, 'src': src, 'dst': dst, 'L0_gnn_label': _L0_gnn_in['label'], 'L0_gnn_W1_l': _L0_gnn_in['W1_l'], 'L0_gnn_W1_r': _L0_gnn_in['W1_r'], 'L0_gnn_b1': _L0_gnn_in['b1'], 'L0_gnn_W2_l': _L0_gnn_in['W2_l'], 'L0_gnn_W2_r': _L0_gnn_in['W2_r'], 'L0_gnn_b2': _L0_gnn_in['b2'], 'L0_mix_w_qkv': _L0_mix_in['w_qkv'], 'L0_mix_proj_mat': _L0_mix_in['proj_mat'], 'L0_mix_w_proj': _L0_mix_in['w_proj'], 'L0_mix_b_proj': _L0_mix_in['b_proj'], 'L0_ffn_Wr': _L0_ffn_in['Wr'], 'L0_ffn_br': _L0_ffn_in['br'], 'L0_ffn_W1': _L0_ffn_in['W1'], 'L0_ffn_b1': _L0_ffn_in['b1'], 'L0_ffn_W2': _L0_ffn_in['W2'], 'L0_ffn_b2': _L0_ffn_in['b2']}

def reference(x, src, dst, L0_gnn_label, L0_gnn_W1_l, L0_gnn_W1_r, L0_gnn_b1, L0_gnn_W2_l, L0_gnn_W2_r, L0_gnn_b2, L0_mix_w_qkv, L0_mix_proj_mat, L0_mix_w_proj, L0_mix_b_proj, L0_ffn_Wr, L0_ffn_br, L0_ffn_W1, L0_ffn_b1, L0_ffn_W2, L0_ffn_b2):
    import jax
    import jax.numpy as jnp

    def _L0_gnn_ref(x, label, edge_index, batch, W1_l, W1_r, b1, W2_l, W2_r, b2):
        import jax, jax.numpy as jnp
        import numpy as np
        N_NODES = 10000
        N_EDGES = 5000
        D_IN = 512
        D_HID = 512
        D_OUT = 512

        def _sage_conv(x, src, dst, W_l, W_r, b):
            n = x.shape[0]
            summed = jax.ops.segment_sum(x[src], dst, num_segments=n)
            deg = jax.ops.segment_sum(jnp.ones((src.shape[0],), x.dtype), dst, num_segments=n)
            agg = summed / jnp.maximum(deg, 1.0)[:, None]
            return agg @ W_l.T + x @ W_r.T + b
        src, dst = (edge_index[0], edge_index[1])
        h = _sage_conv(x, src, dst, W1_l, W1_r, b1)
        h = jnp.tanh(h)
        out = _sage_conv(h, src, dst, W2_l, W2_r, b2)
        return out

    def _L0_mix_ref(x, w_qkv, proj_mat, w_proj, b_proj):
        import jax, jax.numpy as jnp
        import numpy as np
        DIM, HEADS, NB_FEATURES = (512, 8, 64)
        HEAD_DIM = DIM // HEADS

        def _phi(t, proj_mat):
            return jax.nn.elu(jnp.einsum('bnhd,hdf->bnhf', t, proj_mat)) + 1.0
        B, N, dim = x.shape
        H, D = (HEADS, dim // HEADS)
        qkv = x @ w_qkv
        q, k, v = jnp.split(qkv, 3, axis=-1)
        q = q.reshape(B, N, H, D)
        k = k.reshape(B, N, H, D)
        v = v.reshape(B, N, H, D)
        q_phi = _phi(q, proj_mat)
        k_phi = _phi(k, proj_mat)
        kv = jnp.einsum('bnhf,bnhd->bhfd', k_phi, v)
        z = 1.0 / jnp.einsum('bnhf,bhf->bnh', q_phi, k_phi.sum(axis=1))
        out = jnp.einsum('bnhf,bhfd,bnh->bnhd', q_phi, kv, z)
        out = out.reshape(B, N, H * D)
        return out @ w_proj + b_proj

    def _L0_ffn_ref(x, Wr, br, W1, b1, W2, b2):
        import jax, jax.numpy as jnp
        import numpy as np
        B, S, D = (8, 128, 512)
        H = 64
        O = 512
        E = 8
        TOP_K = 1
        b, s, d = x.shape
        xf = x.reshape(-1, d)
        router_logits = xf @ Wr + br
        topk_logits, topk_idx = jax.lax.top_k(router_logits, TOP_K)
        topk_gates = jax.nn.softmax(topk_logits, axis=1)
        out = jnp.zeros((xf.shape[0], O), dtype=x.dtype)
        for k in range(TOP_K):
            idx_k = topk_idx[:, k]
            gate_k = topk_gates[:, k:k + 1]
            for e in range(E):
                h = jax.nn.relu(xf @ W1[e] + b1[e])
                oe = h @ W2[e] + b2[e]
                mask = (idx_k == e)[:, None]
                out = out + jnp.where(mask, gate_k * oe, 0.0)
        return out.reshape(b, s, O)
    edge_index = jnp.stack([src, dst])
    batch0 = jnp.zeros((10000,), jnp.int32)
    xn = _layernorm(x, axis=-1)
    x = x + _L0_gnn_ref(xn, L0_gnn_label, edge_index, batch0, L0_gnn_W1_l, L0_gnn_W1_r, L0_gnn_b1, L0_gnn_W2_l, L0_gnn_W2_r, L0_gnn_b2) + _L0_mix_ref(xn[None], L0_mix_w_qkv, L0_mix_proj_mat, L0_mix_w_proj, L0_mix_b_proj)[0]
    x = x + _L0_ffn_ref(_layernorm(x, axis=-1)[None], L0_ffn_Wr, L0_ffn_br, L0_ffn_W1, L0_ffn_b1, L0_ffn_W2, L0_ffn_b2)[0]
    return x

_drawn_inputs = setup_inputs


def setup_inputs(seed=0):
    import zlib

    import numpy as np

    out = dict(_drawn_inputs(seed))
    spreads = {'L0_gnn_b1': (0.0, 0.1),
     'L0_gnn_b2': (0.0, 0.1),
     'L0_ffn_br': (0.0, 0.1),
     'L0_ffn_b1': (0.0, 0.8),
     'L0_ffn_b2': (0.0, 0.1)}
    factors = {'L0_mix_w_qkv': 3.692,
     'L0_mix_proj_mat': 5.006,
     'L0_mix_w_proj': 3.386,
     'L0_mix_b_proj': 5.449}
    for name, (base, spread) in spreads.items():
        noise = np.random.default_rng([zlib.crc32(name.encode()), seed]).standard_normal(out[name].shape)
        drawn = base * np.exp(spread * noise) if base else spread * noise
        out[name] = jnp.asarray(drawn.astype(out[name].dtype))
    for name, factor in factors.items():
        out[name] = (out[name] * factor).astype(out[name].dtype)
    return out
```

```python
from contextlib import ExitStack

import concourse.bass as bass
from concourse import mybir

P = 128
D = 512
KC = D // P
TG = 4
GROUP = TG * P
N = 10000
NG = 2 * -(-N // (2 * GROUP))
NP = NG * GROUP
NT = NG * TG
PAIRS = NG // 2
TRASH = NP - P
HEADS, HD = 8, 64
EXP, EH = 8, 64
AW = 520
EPS = 1e-5

ALU = mybir.AluOpType
ACT = mybir.ActivationFunctionType
F32 = mybir.dt.float32
I32 = mybir.dt.int32
U32 = mybir.dt.uint32


def need(eng, sem, value):
    if not (isinstance(value, int) and value <= 0):
        eng.wait_ge(sem, value)


def active(t, lag, count):
    return not isinstance(t, int) or 0 <= t - lag < count


def turns(eng, body, tail, head=1):
    for k in range(8 * head):
        body(k // 8, k % 8)
    with eng.Fori(head, PAIRS) as it:
        for k in range(8):
            body(it, k)
    for k in range(tail):
        body(PAIRS, k)


def group_turns(eng, body, tail, head=1):
    for b in range(2 * head):
        body(b // 2, b % 2)
    with eng.Fori(head, PAIRS) as it:
        for b in range(2):
            body(it, b)
    for b in range(tail):
        body(PAIRS + b // 2, b % 2)


def lagged(turn, k, lag, per=8):
    return turn + (k - lag) // per, (k - lag) % per


def build(nc, x, src, dst, w1lT, w1rT, b1, w2lT, w2rT, b2, wqT, wkT, wv, pmat, wproj, bproj,
          wr, br, f1, fb1, f2, fb2, ident_in, tri_in, bmask_in, valid_in, trash_in, expand_in,
          iota_in, out):
    with ExitStack() as ctx:
        def sb(name, shape, dt=F32):
            return ctx.enter_context(nc.sbuf_tensor(name, shape, dt))

        def sem(name):
            return ctx.enter_context(nc.semaphore(name))

        xnT_d = nc.dram_tensor("xnT_d", [NG, P, KC * GROUP], F32)
        hT_d = nc.dram_tensor("hT_d", [NG, P, KC * GROUP], F32)
        agg1_d = nc.dram_tensor("agg1_d", [NP, AW], F32)
        agg2_d = nc.dram_tensor("agg2_d", [NP, D], F32)
        y_d = nc.dram_tensor("y_d", [NP, D], F32)
        part_d = nc.dram_tensor("part_d", [NG, P, TG * D], F32)
        agg1_g = agg1_d.ap().rearrange("(g p j) w -> g p (j w)", p=P, j=TG)
        agg2_g = agg2_d.ap().rearrange("(g p j) w -> g p (j w)", p=P, j=TG)
        y_g = y_d.ap().rearrange("(g p j) w -> g p (j w)", p=P, j=TG)
        x_g = x.rearrange("(g p j) w -> g p (j w)", p=P, j=TG)
        out_g = out.rearrange("(g p j) w -> g p (j w)", p=P, j=TG)
        src_g = src.rearrange("(g p j) -> g p j", p=P, j=TG)
        dst_g = dst.rearrange("(g p j) -> g p j", p=P, j=TG)
        dst_row = dst.rearrange("(g a e) -> g a e", a=1, e=GROUP)

        bank = [ctx.enter_context(nc.psum_tensor(f"bank{i}", [P, D], F32)) for i in range(8)]

        ident = sb("ident", [P, P])
        tri = sb("tri", [P, P])
        bmask = sb("bmask", [P, P])
        valid = sb("valid", [P, NG])
        trash = sb("trash", [P, 1])
        expand = sb("expand", [EXP, KC, P])
        iota8 = sb("iota8", [P, EXP])
        W1l, W1r, W2l, W2r, Wq, Wk = (sb(n, [P, KC, D]) for n in
                                      ("W1l", "W1r", "W2l", "W2r", "Wq", "Wk"))
        M = Wk
        F1, F2 = W1l, W1r
        b1c = sb("b1c", [P, KC])
        fb1c = sb("fb1c", [P, KC])
        fb2s = sb("fb2s", [EXP, D])
        wrs = sb("wrs", [P, KC, EXP])
        brs = sb("brs", [P, EXP])
        bias = sb("bias", [P, D])
        KS = sb("KS", [P, KC, P])
        ksum = sb("ksum", [P, KC])
        rdeg = sb("rdeg", [P, NT])

        R = [sb(f"R{i}", [P, 2, TG * D]) for i in range(5)]
        R5 = sb("R5", [P, 2, TG * AW])

        esrc = sb("esrc", [P, 2, TG], I32)
        edst = sb("edst", [P, 2, TG], I32)
        erow = sb("erow", [P, 2, GROUP], I32)
        dstf = sb("dstf", [P, 2, TG])
        todump = sb("todump", [P, 2, TG])
        G = sb("G", [P, 4, D])
        S = sb("S", [P, 4, P])
        Sj = sb("Sj", [P, P])
        cnt = sb("cnt", [P, 4])
        cnt1 = sb("cnt1", [P, 4])
        eidx = sb("eidx", [P, 4, 1], I32)
        O = sb("O", [P, 4, AW])
        est = sb("est", [P, 6])

        st = sb("st", [P, 6])
        mv = sb("mv", [P, TG, 2])
        veps = sb("veps", [P, TG])
        rs = sb("rs", [P, TG])
        nhalf = sb("nhalf", [P, TG])
        low = sb("low", [P, 2, D])
        phi = sb("phi", [P, 4, D])
        rd = sb("rd", [P, 2, TG])
        pd = sb("pd", [P, D])

        logit = sb("logit", [P, TG * EXP])
        mx = sb("mx", [P, TG, 8])
        ix = sb("ix", [P, TG, 8], U32)
        ixf = sb("ixf", [P, TG])
        topd, tope, gate = sb("topd", [P, TG]), sb("tope", [P, TG]), sb("gate", [P, TG])
        rtop = sb("rtop", [P, TG])
        onehot = sb("onehot", [P, TG, EXP])
        maskT = sb("maskT", [EXP, 2, GROUP])

        s_w = sem("weights_in")
        s_f = sem("expert_weights_in")
        s_z = sem("zeroed")
        s_foldc = sem("fold_copied")
        s_prep = sem("prepared")
        s_phase = sem("phase_done")

        def phase_end(eng, k):
            eng.drain().then_inc(s_phase, 1)
            eng.wait_ge(s_phase, 5 * k)

        def slot(buf, b):
            return buf[:, b, 0:TG * D].rearrange("p (c n) -> p c n", c=TG)

        wqTs, wkTs = slot(R[0], 0), slot(R[0], 1)
        wvs, wps = slot(R[3], 0), slot(R[3], 1)
        blockP = kvT = R[4][:, 0, 0:KC * P].rearrange("p (c f) -> p c f", c=KC)
        K2T = slot(R[4], 1)
        zero = R5[:, 1, :]

        s_past = {}

        def need_apart(eng, sem, value):
            need(eng, sem, value)
            if not isinstance(value, int):
                eng.sem_inc(s_past[eng.engine], 1)

        e_in = [sem(f"edge_lists_in{b}") for b in range(2)]
        e_f = sem("edge_targets_float")
        e_td = sem("edge_trash_offset")
        e_g = [sem(f"edge_gathered{i}") for i in range(4)]
        e_cnt, e_cnt1, e_ix = sem("edge_repeats"), sem("edge_repeated"), sem("edge_rows")
        e_st = sem("edge_stats")
        e_s = sem("edge_tile_ready")
        e_mm = sem("edge_summed")
        e_o = sem("edge_sums_out")
        e_sc = sem("edge_scattered")
        s_z1, s_z2 = sem("agg1_cleared"), sem("agg2_cleared")

        def pair(name):
            return [sem(f"{name}{b}") for b in range(2)]

        a_x, a_st = pair("keys_x_in"), pair("keys_xnT_stored")
        a_s1, a_s2, a_s3 = sem("keys_stats"), sem("keys_mean_var"), sem("keys_rstd")
        a_ve, f_ve = sem("keys_var_eps"), sem("ffn_var_eps")
        a_xn, a_tr, a_ev = sem("keys_xn"), sem("keys_transposed"), sem("keys_xnT")
        a_kp, a_min, a_exp = sem("keys_k"), sem("keys_min"), sem("keys_exp")
        a_phi, a_T = sem("keys_phi"), sem("keys_summed")
        c_k2, c_kv, c_kvc, c_m = sem("fold_k2"), sem("fold_kv"), sem("fold_kv_kept"), sem("fold_m")
        b_xt, b_agg, b_yst, b_hst = (pair(n) for n in ("hid_xnT_in", "hid_agg_in", "hid_y_stored",
                                                       "hid_h_stored"))
        b_d, b_r, b_ag = sem("hid_degree"), sem("hid_rdegree"), sem("hid_mean")
        b_tr, b_ev, b_h, b_th = sem("hid_transposed"), sem("hid_aggT"), sem("hid_h"), sem("hid_tanh")
        b_y, b_yo = sem("hid_y"), sem("hid_y_out")
        m_xt, m_ht, m_x, m_st = (pair(n) for n in ("mix_xnT_in", "mix_hT_in", "mix_x_in",
                                                   "mix_stored"))
        m_q, m_min, m_exp, m_phi = sem("mix_q"), sem("mix_min"), sem("mix_exp"), sem("mix_phi")
        m_den, m_z, m_qz, m_xb = sem("mix_den"), sem("mix_z"), sem("mix_qz"), sem("mix_x_bias")
        m_p, m_po = sem("mix_product"), sem("mix_part")
        f_p, f_a, f_st = pair("ffn_part_in"), pair("ffn_agg_in"), pair("ffn_stored")
        f_rd, f_x2 = sem("ffn_rdegree"), sem("ffn_x2")
        f_s1, f_s2, f_s3 = sem("ffn_stats"), sem("ffn_mean_var"), sem("ffn_rstd")
        f_xn, f_tr, f_ev, f_r = sem("ffn_xn"), sem("ffn_transposed"), sem("ffn_xnT"), sem("ffn_logits")
        f_l, f_mx, f_ix, f_ixf = sem("ffn_logits_b"), sem("ffn_max"), sem("ffn_index"), sem("ffn_indexf")
        f_d, f_e, f_g, f_oh = sem("ffn_top"), sem("ffn_top_exp"), sem("ffn_gate"), sem("ffn_onehot")
        f_rt = sem("ffn_top_reciprocal")
        f_mt, f_mtc, f_h1, f_re = sem("ffn_maskT"), sem("ffn_maskT_kept"), sem("ffn_h"), sem("ffn_relu")
        f_m, f_hm, f_h2, f_out = sem("ffn_mask"), sem("ffn_masked"), sem("ffn_product"), sem("ffn_out")

        for e in (nc.vector, nc.gpsimd):
            s_past[e.engine] = sem(f"wait_passed_{len(s_past)}")

        block = ctx.enter_context(nc.Block())

        def edge_load(sp, ph, turn, b):
            g = 2 * turn + b
            need(sp, e_s, ph * NT + 4 * g - 4)
            for to, of in ((esrc[:, b, :], src_g[g]), (edst[:, b, :], dst_g[g]),
                           (erow[:, b, :], dst_row[g].to_broadcast([P, GROUP]))):
                sp.dma_start(to, of).then_inc(e_in[b], 16)

        def edge_pool(pool, ph, turn, k, table, agg, width):
            t = 8 * turn + k
            if active(t, 0, NT):
                b, j = k // 4, k % 4
                if j == 0:
                    need_apart(pool, e_in[b], 48 * (ph * PAIRS + turn + 1))
                need_apart(pool, e_mm, ph * NT + t - 3)
                pool.indirect_dma_start(G[:, j, :], None, table,
                                        bass.IndirectOffsetOnAxis(ap=esrc[:, b, j:j + 1], axis=0)
                                        ).then_inc(e_g[j], 16)
            if active(t, 2, NT):
                j = (k - 2) % 4
                need_apart(pool, e_o, ph * NT + t - 1)
                need_apart(pool, e_sc, 16 * (ph * NT + t - 2))
                pool.indirect_dma_start(agg, bass.IndirectOffsetOnAxis(ap=eidx[:, j, 0:1], axis=0),
                                        O[:, j, 0:width], None, compute_op=ALU.add).then_inc(e_sc, 16)

        def edge_dve(dve, ph, turn, k, norm):
            t = 8 * turn + k
            if not active(t, 1, NT):
                return
            turn1, kk = lagged(turn, k, 1)
            b, j = kk // 4, kk % 4
            u, ug = ph * NT + t, ph * NG + 2 * turn1 + b
            if j == 0:
                dve.wait_ge(e_in[b], 48 * (ph * PAIRS + turn1 + 1))
                dve.tensor_copy(dstf[:, b, :], edst[:, b, :]).then_inc(e_f, 1)
                dve.wait_ge(e_f, ug + 1)
                dve.tensor_scalar(todump[:, b, :], dstf[:, b, :], -1.0, trash[:, 0:1], ALU.mult, ALU.add
                                  ).then_inc(e_td, 1)
            need(dve, e_mm, u - 4)
            need(dve, e_sc, 16 * (u - 4))
            row = erow[:, b, j:GROUP:TG]
            dve.scalar_tensor_tensor(Sj[:, :], row, dstf[:, b, j:j + 1], tri[:, :], ALU.is_equal,
                                     ALU.mult, accum_out=cnt[:, j:j + 1]).then_inc(e_cnt, 1)
            dve.tensor_scalar(S[:, j, :], row, dstf[:, b, j:j + 1], 0.0, ALU.is_equal, ALU.add,
                              accum_out=O[:, j, D:D + 1])
            dve.wait_ge(e_cnt, u)
            dve.tensor_scalar(cnt1[:, j:j + 1], cnt[:, j:j + 1], 1.0, None, ALU.min).then_inc(e_cnt1, 1)
            dve.wait_ge(e_cnt1, u)
            if j == 0:
                dve.wait_ge(e_td, ug + 1)
            dve.wait_ge(e_g[j], 16 * (ph * NT // 4 + 2 * turn1 + b + 1))
            ix = dve.scalar_tensor_tensor(eidx[:, j, :], cnt1[:, j:j + 1], todump[:, b, j:j + 1],
                                          dstf[:, b, j:j + 1], ALU.mult, ALU.add)
            if norm:
                dve.wait_ge(a_s3, t + 1)
                dve.tensor_scalar(G[:, j, :], G[:, j, :], mv[:, 1, 0:1], rs[:, 1:2], ALU.subtract,
                                  ALU.mult).then_inc(e_s, 1)
            else:
                ix.then_inc(e_s, 1)

        def edge_pe(pe, ph, turn, k, psum):
            t = 8 * turn + k
            if active(t, 2, NT):
                j = (k - 2) % 4
                pe.wait_ge(e_s, ph * NT + t - 1)
                need(pe, e_o, ph * NT + t - 2)
                pe.matmul(psum, S[:, j, :], G[:, j, :], start=True, stop=True).then_inc(e_mm, 1)

        def edge_act(act, ph, turn, k, psum):
            t = 8 * turn + k
            if active(t, 2, NT):
                j = (k - 2) % 4
                act.wait_ge(e_mm, ph * NT + t - 1)
                need(act, e_sc, 16 * (ph * NT + t - 5))
                act.copy(O[:, j, 0:D], psum).then_inc(e_o, 1)

        s_bp = sem("feature_blocks_in")
        k_pe, k_cp = sem("weights_folded"), sem("weights_kept")

        def kpn(w):
            return w.rearrange("(c p) n -> p c n", p=P)

        weights = [(ident[:], ident_in), (tri[:], tri_in), (bmask[:], bmask_in), (valid[:], valid_in),
                   (trash[:], trash_in), (iota8[:], iota_in), (expand[:], expand_in),
                   (wkTs, kpn(wkT)), (wqTs, kpn(wqT)), (W1l[:], kpn(w1lT)), (W1r[:], kpn(w1rT)),
                   (W2l[:], kpn(w2lT)), (W2r[:], kpn(w2rT)), (wvs, kpn(wv)), (wps, kpn(wproj)),
                   (wrs[:], kpn(wr)),
                   (b1c[:], b1), (fb1c[:], fb1), (fb2s[:], fb2), (brs[:], br.to_broadcast([P, EXP])),
                   (bias[:], b2.to_broadcast([P, D])), (pd[:], bproj.to_broadcast([P, D]))]

        @block.sync
        def _(sp):
            for to, of in weights:
                sp.dma_start(to, of).then_inc(s_w, 16)
            sp.wait_ge(s_z, 2)
            for h in range(HEADS):
                o = HD * (h % 2)
                sp.dma_start(blockP[o:o + HD, h // 2, o:o + HD], pmat[h]).then_inc(s_bp, 16)
            phase_end(sp, 1)

            def keys(turn, b):
                g = 2 * turn + b
                need(sp, a_xn, 4 * (g - 1))
                sp.dma_start(R[0][:, b, :], x_g[g]).then_inc(a_x[b], 16)
                edge_load(sp, 0, turn, b)
            group_turns(sp, keys, 0)
            phase_end(sp, 2)

            def hidden(turn, b):
                g = 2 * turn + b
                if active(g, 0, NG):
                    need(sp, b_h, 4 * (g - 1))
                    sp.dma_start(R[0][:, b, :], xnT_d[g]).then_inc(b_xt[b], 16)
                    need(sp, b_tr, 4 * (g - 1))
                    sp.dma_start(R5[:, b, :], agg1_g[g]).then_inc(b_agg[b], 16)
                if active(g, 1, NG):
                    sp.wait_ge(b_yo, 4 * g)
                    sp.dma_start(y_g[g - 1], R[4][:, 1 - b, :]).then_inc(b_yst[1 - b], 16)
            group_turns(sp, hidden, 1)
            for b in range(2):
                sp.wait_ge(b_yst[b], 16 * PAIRS)
            phase_end(sp, 3)

            sp.dma_start(F1[:], kpn(f1)).then_inc(s_f, 16)
            sp.dma_start(F2[:], kpn(f2)).then_inc(s_f, 16)

            def mix(turn, b):
                g = 2 * turn + b
                if active(g, 0, NG):
                    need(sp, m_q, 4 * (g - 1))
                    sp.dma_start(R[0][:, b, :], xnT_d[g]).then_inc(m_xt[b], 16)
                    edge_load(sp, 1, turn, b)
                if active(g, 1, NG):
                    turn1, b1_ = lagged(turn, b, 1, 2)
                    need(sp, m_p, 4 * (g - 2))
                    sp.dma_start(R[1][:, b1_, :], hT_d[g - 1]).then_inc(m_ht[b1_], 16)
                    need(sp, m_po, 4 * (g - 2))
                    sp.dma_start(R[2][:, b1_, :], x_g[g - 1]).then_inc(m_x[b1_], 16)
                if active(g, 3, NG):
                    sp.wait_ge(m_po, 4 * (g - 2))
                    sp.dma_start(part_d[g - 3], R[4][:, 1 - b, :]).then_inc(m_st[1 - b], 16)
            group_turns(sp, mix, 3, head=2)
            for b in range(2):
                sp.wait_ge(m_st[b], 16 * PAIRS)
            phase_end(sp, 4)

            def ffn(turn, b):
                g = 2 * turn + b
                if active(g, 0, NG):
                    need(sp, f_st[b], 16 * turn)
                    sp.dma_start(R[0][:, b, :], part_d[g]).then_inc(f_p[b], 16)
                    need(sp, f_tr, 4 * (g - 1))
                    sp.dma_start(R[1][:, b, :], agg2_g[g]).then_inc(f_a[b], 16)
                if active(g, 1, NG):
                    sp.wait_ge(f_out, 4 * g)
                    sp.dma_start(out_g[g - 1], R[0][:, 1 - b, :]).then_inc(f_st[1 - b], 16)
            group_turns(sp, ffn, 1)
            for b in range(2):
                sp.wait_ge(f_st[b], 16 * PAIRS)

        @block.gpsimd
        def _(pool):
            pool.memset(zero, 0.0).then_inc(s_z, 1)
            pool.memset(blockP, 0.0).then_inc(s_z, 1)
            pool.memset(nhalf[:, :], -0.5)
            pool.memset(O[:, :, :], 0.0)
            pool.memset(mv[:, :, :], 1.0)
            pool.wait_ge(s_w, 16 * len(weights))
            pool.tensor_tensor(bias[:, :], bias[:, :], pd[:, :], ALU.add).then_inc(s_prep, 1)
            phase_end(pool, 1)
            pool.wait_ge(s_z1, 16 * NG)

            def keys(turn, k):
                t = 8 * turn + k
                if active(t, 0, NT + 1):
                    need_apart(pool, a_s2, t + 1)
                    pool.tensor_scalar(veps[:, 0:2], mv[:, 0:2, 1], EPS, None, ALU.add).then_inc(a_ve, 1)
                    pool.wait_ge(a_ve, t + 1)
                    pool.tensor_tensor(rs[:, 0:2], veps[:, 0:2], nhalf[:, 0:2], ALU.pow).then_inc(a_s3, 1)
                edge_pool(pool, 0, turn, k, x, agg1_d.ap(), AW)
            turns(pool, keys, 2)
            pool.wait_ge(e_sc, 16 * NT)
            phase_end(pool, 2)
            phase_end(pool, 3)
            pool.wait_ge(s_z2, 16 * NG)

            def step(turn, k):
                t = 8 * turn + k
                edge_pool(pool, 1, turn, k, y_d.ap(), agg2_d.ap(), D)
                if active(t, 6, NT):
                    turn1, kk = lagged(turn, k, 6)
                    b, j = kk // 4, kk % 4
                    if j == 0:
                        pool.wait_ge(m_x[b], 16 * (turn1 + 1))
                    xr = slot(R[2], b)[:, j, :]
                    pool.tensor_tensor(xr, xr, bias[:, :], ALU.add).then_inc(m_xb, 1)
            turns(pool, step, 6)
            pool.wait_ge(e_sc, 16 * 2 * NT)
            phase_end(pool, 4)

            def ffn(turn, b):
                for j in range(TG):
                    t = 4 * (2 * turn + b) + j
                    need_apart(pool, f_s2, t + 1)
                    pool.tensor_scalar(veps[:, j:j + 1], mv[:, j, 1:2], EPS, None, ALU.add
                                       ).then_inc(f_ve, 1)
                    pool.wait_ge(f_ve, t + 1)
                    pool.tensor_tensor(rs[:, j:j + 1], veps[:, j:j + 1], nhalf[:, j:j + 1], ALU.pow
                                       ).then_inc(f_s3, 1)
            group_turns(pool, ffn, 0)

        @block.scalar
        def _(act):
            act.wait_ge(s_z, 1)
            for g in range(NG):
                act.dma_start(agg1_g[g], zero).then_inc(s_z1, 16)
            for g in range(NG):
                act.dma_start(agg2_g[g], zero[:, 0:TG * D]).then_inc(s_z2, 16)
            phase_end(act, 1)

            def keys(turn, k):
                t, b, j = 8 * turn + k, k // 4, k % 4
                if active(t, 0, NT):
                    act.wait_ge(a_tr, t + 1)
                    if j == 0:
                        need(act, a_kp, t - 4)
                        need(act, a_st[b], 16 * turn)
                    act.copy(slot(R[2], b)[:, :, j * P:(j + 1) * P],
                             bank[5][:, :].rearrange("p (c n) -> p c n", c=KC)).then_inc(a_ev, 1)
                if active(t, 1, NT):
                    act.wait_ge(a_min, t)
                    lo = low[:, (k - 1) % 2, :]
                    act.activation(lo, lo, ACT.Exp).then_inc(a_exp, 1)
                edge_act(act, 0, turn, k, bank[7][:, :])
                if active(t, 0, NT) and j == 3:
                    act.wait_ge(a_ev, t + 1)
                    act.dma_start(xnT_d[2 * turn + b], R[2][:, b, :]).then_inc(a_st[b], 16)
            turns(act, keys, 2)
            for b in range(2):
                act.wait_ge(a_st[b], 16 * PAIRS)
            act.wait_ge(s_z2, 16 * NG)
            phase_end(act, 2)

            def hidden(turn, b):
                g = 2 * turn + b
                for j in range(TG):
                    act.wait_ge(b_tr, 4 * g + j + 1)
                    if j == 0:
                        need(act, b_h, 4 * (g - 1))
                    act.copy(slot(R[1], b)[:, :, j * P:(j + 1) * P],
                             bank[j % 2][:, :].rearrange("p (c n) -> p c n", c=KC)).then_inc(b_ev, 1)
                for o in range(KC):
                    act.wait_ge(b_h, 4 * g + o + 1)
                    if o == 0:
                        need(act, b_y, 4 * (g - 1))
                        need(act, b_hst[b], 16 * turn)
                    act.activation(slot(R[2], b)[:, o, :], bank[2 + o % 2][:, :], ACT.Tanh,
                                   bias=b1c[:, o:o + 1]).then_inc(b_th, 1)
                act.wait_ge(b_th, 4 * g + 4)
                act.dma_start(hT_d[g], R[2][:, b, :]).then_inc(b_hst[b], 16)
            group_turns(act, hidden, 0)
            for b in range(2):
                act.wait_ge(b_hst[b], 16 * PAIRS)
            phase_end(act, 3)

            def mix(turn, k):
                t = 8 * turn + k
                if active(t, 1, NT):
                    act.wait_ge(m_min, t)
                    lo = low[:, (k - 1) % 2, :]
                    act.activation(lo, lo, ACT.Exp).then_inc(m_exp, 1)
                edge_act(act, 1, turn, k, bank[7][:, :])
            turns(act, mix, 2)
            phase_end(act, 4)

            def ffn(turn, b):
                g = 2 * turn + b
                if active(g, 1, NG):
                    b1_ = 1 - b
                    act.wait_ge(f_d, g)
                    act.activation(tope[:, :], topd[:, :], ACT.Exp).then_inc(f_e, 1)
                    for c in range(KC):
                        act.wait_ge(f_h1, 4 * (g - 1) + c + 1)
                        if c == 0:
                            need(act, f_h2, 4 * (g - 2))
                        act.activation(slot(R[4], b1_)[:, c, :], bank[2 + c % 2][:, :], ACT.Relu,
                                       bias=fb1c[:, c:c + 1]).then_inc(f_re, 1)
                        if c == 1:
                            act.wait_ge(f_mt, g)
                            act.copy(maskT[:, b1_, :], bank[5][0:EXP, :]).then_inc(f_mtc, 1)
                if active(g, 0, NG):
                    for j in range(TG):
                        act.wait_ge(f_tr, 4 * g + j + 1)
                        if j == 0:
                            need(act, f_h1, 4 * (g - 1))
                        act.copy(slot(R[3], b)[:, :, j * P:(j + 1) * P],
                                 bank[j % 2][:, :].rearrange("p (c n) -> p c n", c=KC)
                                 ).then_inc(f_ev, 1)
            group_turns(act, ffn, 1, head=2)

        @block.vector
        def _(dve):
            for i in range(2 * KC):
                dve.wait_ge(k_pe, i + 1)
                dve.tensor_copy((Wk if i < KC else Wq)[:, i % KC, :], bank[i][:, :]).then_inc(k_cp, 1)
            phase_end(dve, 1)

            def keys(turn, k):
                t, b, j = 8 * turn + k, k // 4, k % 4
                if active(t, 0, NT):
                    if j == 0:
                        dve.wait_ge(a_x[b], 16 * (turn + 1))
                    xr = slot(R[0], b)[:, j, :]
                    dve.bn_stats(st[:, :], xr).then_inc(a_s1, 1)
                if active(t, 1, NT):
                    turn1, kk = lagged(turn, k, 1)
                    dve.wait_ge(e_g[kk % 4], 16 * (2 * turn1 + kk // 4 + 1))
                    dve.bn_stats(est[:, :], G[:, kk % 4, :]).then_inc(e_st, 1)
                if active(t, 0, NT):
                    need_apart(dve, a_s1, t + 1)
                    last = dve.bn_aggr(mv[:, 0, :], st[:, :])
                if active(t, 1, NT):
                    need_apart(dve, e_st, t)
                    last = dve.bn_aggr(mv[:, 1, :], est[:, :])
                last.then_inc(a_s2, 1)
                if active(t, 0, NT):
                    dve.wait_ge(a_s3, t + 1)
                    need(dve, a_T, t - 7)
                    dve.tensor_scalar(slot(R[1], b)[:, j, :], xr, mv[:, 0, 0:1], rs[:, 0:1],
                                      ALU.subtract, ALU.mult).then_inc(a_xn, 1)
                edge_dve(dve, 0, turn, k, True)
                if active(t, 1, NT):
                    lo = low[:, (k - 1) % 2, :]
                    dve.wait_ge(a_kp, t)
                    dve.tensor_scalar(lo, bank[6][:, :], 0.0, None, ALU.min).then_inc(a_min, 1)
                    dve.wait_ge(a_exp, t)
                    need(dve, a_T, t - 4)
                    dve.scalar_tensor_tensor(phi[:, (k - 1) % 4, :], bank[6][:, :], 0.0, lo, ALU.max,
                                             ALU.add).then_inc(a_phi, 1)
            turns(dve, keys, 1)
            phase_end(dve, 2)

            for i in range(KC):
                dve.tensor_copy(K2T[:, i, :], bank[i][:, :]).then_inc(c_k2, 1)
            dve.tensor_copy(ksum[:, :], bank[4][:, 0:KC]).then_inc(c_k2, 1)
            dve.wait_ge(c_k2, KC + 1)
            for c in range(KC):
                dve.tensor_scalar(KS[:, c, :], bmask[:, :], ksum[:, c:c + 1], None, ALU.mult)
            for c in range(KC):
                dve.wait_ge(c_kv, c + 1)
                dve.tensor_tensor(kvT[:, c, :], bank[4 + c][:, 0:P], bmask[:, :], ALU.mult
                                  ).then_inc(c_kvc, 1)
            for c in range(KC):
                dve.wait_ge(c_m, c + 1)
                dve.tensor_copy(M[:, c, :], bank[c][:, :]).then_inc(s_foldc, 1)

            def hidden(turn, b):
                g = 2 * turn + b
                agg = R5[:, b, :].rearrange("p (j w) -> p j w", j=TG)
                if active(g, 0, NG):
                    dve.wait_ge(b_agg[b], 16 * (turn + 1))
                    dve.tensor_scalar(rd[:, b, :], agg[:, :, D], 1.0, None, ALU.max).then_inc(b_d, 1)
                    dve.wait_ge(b_d, g + 1)
                    dve.reciprocal(rd[:, b, :], rd[:, b, :]).then_inc(b_r, 1)
                    dve.wait_ge(b_r, g + 1)
                    dve.tensor_copy(rdeg[:, bass.ds(4 * g, TG)], rd[:, b, :])
                    for j in range(TG):
                        dve.tensor_scalar(agg[:, j, 0:D], agg[:, j, 0:D], rd[:, b, j:j + 1], None,
                                          ALU.mult).then_inc(b_ag, 1)
                if active(g, 1, NG):
                    turn1, b1_ = lagged(turn, b, 1, 2)
                    need(dve, b_yst[b1_], 16 * turn1)
                    for j in range(TG):
                        dve.wait_ge(b_y, 4 * (g - 1) + j + 1)
                        dve.tensor_copy(slot(R[4], b1_)[:, j, :], bank[4 + j % 2][:, :]).then_inc(b_yo, 1)
            group_turns(dve, hidden, 1, head=2)
            phase_end(dve, 3)

            def mix(turn, k):
                t = 8 * turn + k
                if active(t, 1, NT):
                    lo, pq = low[:, (k - 1) % 2, :], bank[(k - 1) % 2][:, :]
                    dve.wait_ge(m_q, t)
                    dve.tensor_scalar(lo, pq, 0.0, None, ALU.min).then_inc(m_min, 1)
                    dve.wait_ge(m_exp, t)
                    need(dve, m_den, t - 4)
                    dve.scalar_tensor_tensor(phi[:, (k - 1) % 4, :], pq, 0.0, lo, ALU.max, ALU.add
                                             ).then_inc(m_phi, 1)
                if active(t, 3, NT):
                    turn1, kk = lagged(turn, k, 3)
                    dve.wait_ge(m_den, t - 2)
                    need(dve, m_qz, t - 3)
                    dve.reciprocal(pd[:, :], bank[2][:, :]).then_inc(m_z, 1)
                    dve.wait_ge(m_z, t - 2)
                    need(dve, m_p, 4 * (2 * turn1 + kk // 4 - 1))
                    dve.tensor_tensor(slot(R[3], kk // 4)[:, kk % 4, :], phi[:, kk % 4, :], pd[:, :],
                                      ALU.mult).then_inc(m_qz, 1)
                edge_dve(dve, 1, turn, k, False)
                if active(t, 8, NT):
                    turn1, kk = lagged(turn, k, 8)
                    b, j = kk // 4, kk % 4
                    dve.wait_ge(m_p, t - 7)
                    dve.wait_ge(m_xb, t - 7)
                    if j == 0:
                        need(dve, m_st[b], 16 * turn1)
                    dve.tensor_tensor(slot(R[4], b)[:, j, :], bank[4 + j % 2][:, :],
                                      slot(R[2], b)[:, j, :], ALU.add).then_inc(m_po, 1)
            turns(dve, mix, 8, head=2)
            phase_end(dve, 4)

            def ffn(turn, b):
                g = 2 * turn + b
                b1_ = 1 - b
                lg = logit[:, :].rearrange("p (j e) -> p j e", j=TG)

                def pre(j):
                    if not active(g, 0, NG):
                        return
                    x2, xn = slot(R[0], b)[:, j, :], slot(R[1], b)[:, j, :]
                    t = 4 * g + j
                    if j == 0:
                        dve.wait_ge(f_p[b], 16 * (turn + 1))
                        dve.wait_ge(f_a[b], 16 * (turn + 1))
                        dve.tensor_copy(rd[:, b, :], rdeg[:, bass.ds(4 * g, TG)]).then_inc(f_rd, 1)
                        dve.wait_ge(f_rd, g + 1)
                    dve.scalar_tensor_tensor(x2, xn, rd[:, b, j:j + 1], x2, ALU.mult, ALU.add
                                             ).then_inc(f_x2, 1)
                    dve.wait_ge(f_x2, t + 1)
                    dve.bn_stats(st[:, :], x2).then_inc(f_s1, 1)
                    need_apart(dve, f_s1, t + 1)
                    dve.bn_aggr(mv[:, j, :], st[:, :]).then_inc(f_s2, 1)

                def normalise(j):
                    if active(g, 0, NG):
                        dve.wait_ge(f_s3, 4 * g + j + 1)
                        dve.tensor_scalar(slot(R[1], b)[:, j, :], slot(R[0], b)[:, j, :], mv[:, j, 0:1],
                                          rs[:, j:j + 1], ALU.subtract, ALU.mult).then_inc(f_xn, 1)

                if active(g, 1, NG):
                    dve.wait_ge(f_r, g)
                    for j in range(TG):
                        ins = dve.tensor_tensor(lg[:, j, :], bank[5][:, j * EXP:(j + 1) * EXP], brs[:, :],
                                                ALU.add)
                    ins.then_inc(f_l, 1)
                    need_apart(dve, f_l, g)
                    for j in range(TG):
                        ins = dve.max(mx[:, j, :], lg[:, j, :])
                    ins.then_inc(f_mx, 1)
                    dve.wait_ge(f_mx, g)
                    dve.tensor_tensor(topd[:, :], mx[:, :, 0], mx[:, :, 0], ALU.subtract).then_inc(f_d, 1)
                    for j in range(TG):
                        ins = dve.max_index(ix[:, j, :], mx[:, j, :], lg[:, j, :])
                    ins.then_inc(f_ix, 1)
                    dve.wait_ge(f_ix, g)
                    dve.tensor_copy(ixf[:, :], ix[:, :, 0]).then_inc(f_ixf, 1)
                    dve.wait_ge(f_e, g)
                    dve.reciprocal(rtop[:, :], tope[:, :]).then_inc(f_rt, 1)
                    dve.wait_ge(f_rt, g)
                    dve.tensor_tensor(gate[:, :], tope[:, :], rtop[:, :], ALU.mult).then_inc(f_g, 1)
                    dve.wait_ge(f_g, g)
                    dve.wait_ge(f_ixf, g)
                    for j in range(TG):
                        ins = dve.tensor_scalar(onehot[:, j, :], iota8[:, :], ixf[:, j:j + 1],
                                                gate[:, j:j + 1], ALU.is_equal, ALU.mult)
                    ins.then_inc(f_oh, 1)
                for c in range(KC):
                    pre(c)
                    if active(g, 1, NG):
                        dve.wait_ge(f_re, 4 * (g - 1) + c + 1)
                        dve.wait_ge(f_m, 4 * (g - 1) + c + 1)
                        hm = slot(R[4], b1_)[:, c, :]
                        dve.tensor_tensor(hm, hm, bank[4][:, :], ALU.mult).then_inc(f_hm, 1)
                    normalise(c)
                if active(g, 1, NG):
                    for j in range(TG):
                        dve.wait_ge(f_h2, 4 * (g - 1) + j + 1)
                        x2 = slot(R[0], b1_)[:, j, :]
                        dve.tensor_tensor(x2, bank[6 + j % 2][:, :], x2, ALU.add).then_inc(f_out, 1)
            group_turns(dve, ffn, 1)

        @block.tensor
        def _(pe):
            pe.wait_ge(s_w, 16 * len(weights))
            pe.wait_ge(s_bp, 16 * HEADS)
            for i in range(2 * KC):
                w = wkTs if i < KC else wqTs
                for c in range(KC):
                    last = pe.matmul(bank[i][:, c * P:(c + 1) * P], w[:, c, (i % KC) * P:(i % KC + 1) * P],
                                     blockP[:, c, :], start=True, stop=True)
                last.then_inc(k_pe, 1)
            phase_end(pe, 1)

            def product(out_, lhs, rhs, start=True, stop=True):
                for c in range(KC):
                    last = pe.matmul(out_, lhs(c), rhs(c), start=start and c == 0,
                                     stop=stop and c == KC - 1)
                return last

            def turn_tile(psum, row):
                for c in range(KC):
                    last = pe.transpose(psum[:, c * P:(c + 1) * P], row[:, c * P:(c + 1) * P], ident[:, :])
                return last

            def keys(turn, k):
                t, b, j = 8 * turn + k, k // 4, k % 4
                if active(t, 0, NT):
                    pe.wait_ge(a_xn, t + 1)
                    need(pe, a_ev, t)
                    turn_tile(bank[5], slot(R[1], b)[:, j, :]).then_inc(a_tr, 1)
                edge_pe(pe, 0, turn, k, bank[7][:, :])
                if active(t, 2, NT):
                    turn2, kk = lagged(turn, k, 2)
                    xn, ph = slot(R[1], kk // 4)[:, kk % 4, :], phi[:, kk % 4, :]
                    first = isinstance(t, int) and t == 2
                    final = isinstance(t, int) and t == NT + 1
                    pe.wait_ge(a_phi, t - 1)
                    for c in range(KC):
                        pe.matmul(bank[c][:, :], xn[:, c * P:(c + 1) * P], ph, start=first, stop=final,
                                  skip_group_check=True)
                    for c in range(KC):
                        last = pe.matmul(bank[4][:, c:c + 1], ph[:, c * P:(c + 1) * P],
                                         valid[:, bass.ds(2 * turn2 + kk // 4, 1)],
                                         start=first and c == 0, stop=final, skip_group_check=True)
                    last.then_inc(a_T, 1)
                if active(t, 0, NT):
                    pe.wait_ge(a_ev, t + 1)
                    need(pe, a_phi, t)
                    xT = slot(R[2], b)
                    product(bank[6][:, :], lambda c: xT[:, c, j * P:(j + 1) * P],
                            lambda c: Wk[:, c, :]).then_inc(a_kp, 1)
            turns(pe, keys, 2)
            phase_end(pe, 2)

            pe.wait_ge(c_k2, KC + 1)
            for c in range(KC):
                product(bank[4 + c][:, 0:P], lambda i: wvs[:, i, c * P:(c + 1) * P],
                        lambda i: K2T[:, i, c * P:(c + 1) * P]).then_inc(c_kv, 1)
            for c in range(KC):
                pe.wait_ge(c_kvc, c + 1)
                pe.matmul(bank[c][:, :], kvT[:, c, :], wps[:, c, :], start=True, stop=True
                          ).then_inc(c_m, 1)
            pe.wait_ge(s_foldc, KC)

            def hidden(turn, b):
                g = 2 * turn + b
                xT, aT = slot(R[0], b), slot(R[1], b)
                if active(g, 0, NG):
                    for j in range(TG):
                        pe.wait_ge(b_ag, 4 * g + j + 1)
                        need(pe, b_ev, 4 * g + j - 1)
                        turn_tile(bank[j % 2], R5[:, b, j * AW:j * AW + D]).then_inc(b_tr, 1)
                if active(g, 1, NG):
                    hT = slot(R[2], 1 - b)
                    pe.wait_ge(b_th, 4 * g)
                    for j in range(TG):
                        need(pe, b_yo, 4 * (g - 1) + j - 1)
                        product(bank[4 + j % 2][:, :], lambda c: hT[:, c, j * P:(j + 1) * P],
                                lambda c: W2l[:, c, :]).then_inc(b_y, 1)
                if active(g, 0, NG):
                    pe.wait_ge(b_xt[b], 16 * (turn + 1))
                    pe.wait_ge(b_ev, 4 * (g + 1))
                    for o in range(KC):
                        need(pe, b_th, 4 * g + o - 1)
                        ph = bank[2 + o % 2][:, :]
                        product(ph, lambda c: W1r[:, c, o * P:(o + 1) * P], lambda c: xT[:, c, :],
                                stop=False)
                        product(ph, lambda c: W1l[:, c, o * P:(o + 1) * P], lambda c: aT[:, c, :],
                                start=False).then_inc(b_h, 1)
            group_turns(pe, hidden, 1)
            phase_end(pe, 3)

            def mix(turn, k):
                t, b, j = 8 * turn + k, k // 4, k % 4
                if active(t, 0, NT):
                    if j == 0:
                        pe.wait_ge(m_xt[b], 16 * (turn + 1))
                    need(pe, m_phi, t - 1)
                    xT = slot(R[0], b)
                    product(bank[j % 2][:, :], lambda c: Wq[:, c, j * P:(j + 1) * P],
                            lambda c: xT[:, c, :]).then_inc(m_q, 1)
                edge_pe(pe, 1, turn, k, bank[7][:, :])
                if active(t, 7, NT):
                    turn7, kk = lagged(turn, k, 7)
                    b7, j7 = kk // 4, kk % 4
                    if j7 == 0:
                        pe.wait_ge(m_ht[b7], 16 * (turn7 + 1))
                        pe.wait_ge(m_qz, t - 7 + 4)
                    need(pe, m_po, t - 8)
                    hT, qz, pp = slot(R[1], b7), slot(R[3], b7), bank[4 + j7 % 2][:, :]
                    product(pp, lambda c: hT[:, c, j7 * P:(j7 + 1) * P], lambda c: W2r[:, c, :],
                            stop=False)
                    product(pp, lambda c: qz[:, c, j7 * P:(j7 + 1) * P], lambda c: M[:, c, :],
                            start=False).then_inc(m_p, 1)
                if active(t, 2, NT):
                    j2 = (k - 2) % 4
                    pe.wait_ge(m_phi, t - 1)
                    need(pe, m_z, t - 2)
                    pe.matmul(bank[2][:, :], KS[:, j2, :], phi[:, j2, :], start=True, stop=True
                              ).then_inc(m_den, 1)
            turns(pe, mix, 7, head=2)
            phase_end(pe, 4)

            pe.wait_ge(s_f, 32)

            def ffn(turn, b):
                g = 2 * turn + b
                b1_ = 1 - b

                def first_layer(c):
                    need(pe, f_re, 4 * (g - 1) + c - 1)
                    product(bank[2 + c % 2][:, :], lambda i: F1[:, i, c * P:(c + 1) * P],
                            lambda i: slot(R[3], b1_)[:, i, :]).then_inc(f_h1, 1)

                def mask(c):
                    need(pe, f_hm, 4 * (g - 1) + c)
                    pe.matmul(bank[4][:, :], expand[:, c, :], maskT[:, b1_, :], start=True, stop=True
                              ).then_inc(f_m, 1)

                if active(g, 1, NG):
                    pe.wait_ge(f_ev, 4 * g)
                    need(pe, f_mtc, g - 1)
                    for j in range(TG):
                        last = product(bank[5][:, j * EXP:(j + 1) * EXP],
                                       lambda c: slot(R[3], b1_)[:, c, j * P:(j + 1) * P],
                                       lambda c: wrs[:, c, :])
                    last.then_inc(f_r, 1)
                    first_layer(0)
                    first_layer(1)
                    pe.wait_ge(f_oh, g)
                    for j in range(TG):
                        last = pe.transpose(bank[5][0:EXP, j * P:(j + 1) * P], onehot[:, j, :], ident[:, :])
                    last.then_inc(f_mt, 1)
                    first_layer(2)
                    pe.wait_ge(f_mtc, g)
                    mask(0)
                    first_layer(3)
                    for c in range(1, KC):
                        mask(c)
                if active(g, 0, NG):
                    for j in range(TG):
                        pe.wait_ge(f_xn, 4 * g + j + 1)
                        need(pe, f_ev, 4 * g + j - 1)
                        turn_tile(bank[j % 2], slot(R[1], b)[:, j, :]).then_inc(f_tr, 1)
                if active(g, 1, NG):
                    pe.wait_ge(f_hm, 4 * g)
                    hm = slot(R[4], b1_)
                    for j in range(TG):
                        need(pe, f_out, 4 * (g - 1) + j - 1)
                        po = bank[6 + j % 2][:, :]
                        product(po, lambda c: hm[:, c, j * P:(j + 1) * P], lambda c: F2[:, c, :], stop=False)
                        pe.matmul(po, maskT[:, b1_, j * P:(j + 1) * P], fb2s[:, :], start=False, stop=True
                                  ).then_inc(f_h2, 1)
            group_turns(pe, ffn, 1)


def kernel(x, src, dst, L0_gnn_label, L0_gnn_W1_l, L0_gnn_W1_r, L0_gnn_b1, L0_gnn_W2_l, L0_gnn_W2_r,
           L0_gnn_b2, L0_mix_w_qkv, L0_mix_proj_mat, L0_mix_w_proj, L0_mix_b_proj, L0_ffn_Wr, L0_ffn_br,
           L0_ffn_W1, L0_ffn_b1, L0_ffn_W2, L0_ffn_b2):
    import numpy as np
    import concourse.bacc as bacc
    from concourse.bass_utils import run_bass_kernel_spmd

    def lay(a):
        return np.ascontiguousarray(a)

    p = np.arange(P)
    xp = np.zeros((NP, D), np.float32)
    xp[:N] = x
    srcp = np.zeros(NP, np.int32)
    srcp[:N] = src
    dstp = (TRASH + np.arange(NP) // TG % P).astype(np.int32)
    dstp[:N] = dst
    qkv = np.asarray(L0_mix_w_qkv)
    node = GROUP * np.arange(NG)[None, :] + TG * p[:, None]
    arrays = {
        "x": xp, "src": srcp, "dst": dstp,
        "w1lT": lay(np.asarray(L0_gnn_W1_l).T), "w1rT": lay(np.asarray(L0_gnn_W1_r).T),
        "b1": lay(np.asarray(L0_gnn_b1).reshape(KC, P).T),
        "w2lT": lay(np.asarray(L0_gnn_W2_l).T), "w2rT": lay(np.asarray(L0_gnn_W2_r).T),
        "b2": lay(L0_gnn_b2).reshape(1, D),
        "wqT": lay(qkv[:, 0:D].T), "wkT": lay(qkv[:, D:2 * D].T), "wv": lay(qkv[:, 2 * D:3 * D]),
        "pmat": lay(L0_mix_proj_mat), "wproj": lay(L0_mix_w_proj),
        "bproj": lay(L0_mix_b_proj).reshape(1, D),
        "wr": lay(L0_ffn_Wr), "br": lay(L0_ffn_br).reshape(1, EXP),
        "f1": lay(np.asarray(L0_ffn_W1).transpose(1, 0, 2)).reshape(D, EXP * EH),
        "fb1": lay(np.asarray(L0_ffn_b1).reshape(KC, P).T),
        "f2": lay(L0_ffn_W2).reshape(EXP * EH, D), "fb2": lay(L0_ffn_b2),
        "ident_in": np.eye(P, dtype=np.float32),
        "tri_in": (p[None, :] < p[:, None]).astype(np.float32),
        "bmask_in": (p[None, :] // HD == p[:, None] // HD).astype(np.float32),
        "valid_in": (node < N).astype(np.float32),
        "trash_in": (TRASH + p[:, None]).astype(np.float32),
        "expand_in": (np.arange(EXP * EH).reshape(1, KC, P) // EH
                      == np.arange(EXP)[:, None, None]).astype(np.float32),
        "iota_in": np.tile(np.arange(EXP, dtype=np.float32), (P, 1)),
    }
    nc = bacc.Bacc("TRN2", target_bir_lowering=False, num_devices=1)
    feeds, args = {}, {}
    for name, a in arrays.items():
        feeds["in_" + name] = a
        args[name] = nc.dram_tensor("in_" + name, a.shape, mybir.dt.from_np(a.dtype),
                                    kind="ExternalInput").ap()
    out = nc.dram_tensor("out", (NP, D), F32, kind="ExternalOutput").ap()
    build(nc, out=out, **args)
    got = run_bass_kernel_spmd(nc, [feeds], core_ids=[0])
    return got.results[0]["out"][:N]
```

```python
from contextlib import ExitStack

import concourse.bass as bass
from concourse import mybir

P = 128
D = 512
KC = D // P
TG = 4
GROUP = TG * P
N = 10000
NG = 4 * -(-N // (4 * GROUP))
NP = NG * GROUP
NT = NG * TG
PAIRS = NG // 2
TRASH = NP - P
HEADS, HD = 8, 64
EXP, EH = 8, 64
SLOTS = 21
AW = 520
EPS = 1e-5

ALU = mybir.AluOpType
ACT = mybir.ActivationFunctionType
F32 = mybir.dt.float32
F32R = mybir.dt.float32r
I32 = mybir.dt.int32
U32 = mybir.dt.uint32


def need(eng, sem, value):
    if not (isinstance(value, int) and value <= 0):
        eng.wait_ge(sem, value)


def active(t, lag, count):
    return not isinstance(t, int) or 0 <= t - lag < count


def turns(eng, body, tail, head=1, last=0):
    for k in range(8 * head):
        body(k // 8, k % 8)
    with eng.Fori(head, PAIRS - last) as it:
        for k in range(8):
            body(it, k)
    for k in range(8 * last):
        body(PAIRS - last + k // 8, k % 8)
    for k in range(tail):
        body(PAIRS, k)


def group_turns(eng, body, tail, head=1):
    for b in range(2 * head):
        body(b // 2, b % 2)
    with eng.Fori(head, PAIRS) as it:
        for b in range(2):
            body(it, b)
    for b in range(tail):
        body(PAIRS + b // 2, b % 2)


def quad_turns(eng, body, tail, last=0):
    for k in range(4):
        body(0, k)
    with eng.Fori(1, NG // 4 - last) as it:
        for k in range(4):
            body(it, k)
    for k in range(4 * last):
        body(NG // 4 - last + k // 4, k % 4)
    for k in range(tail):
        body(NG // 4, k)


def lagged(turn, k, lag, per=8):
    return turn + (k - lag) // per, (k - lag) % per


def build(nc, x, src, dst, w1lT, w1rT, b1, w2lT, w2rT, b2, wqT, wkT, wv, pmat, wproj, bproj,
          wr, br, f1, fb1, f2, fb2, ident_in, tri_in, bmask_in, valid_in, trash_in, expand_in,
          iota_in, out):
    with ExitStack() as ctx:
        def sb(name, shape, dt=F32):
            return ctx.enter_context(nc.sbuf_tensor(name, shape, dt))

        def sem(name):
            return ctx.enter_context(nc.semaphore(name))

        xnT_d = [nc.dram_tensor(f"xnT_{n}_d", [NG, P, KC * GROUP], F32) for n in ("high", "low")]
        hT_d = [nc.dram_tensor(f"hT_{n}_d", [NG, P, KC * GROUP], F32) for n in ("high", "low")]
        wq_d, w2r_d, m_d, f1_d, f2_d = (
            [nc.dram_tensor(f"{w}_{n}_d", [P, KC * D], F32) for n in ("high", "low")]
            for w in ("wq", "w2r", "m", "f1", "f2"))
        agg1_d = nc.dram_tensor("agg1_d", [NP, AW], F32)
        agg2_d = nc.dram_tensor("agg2_d", [NP, D], F32)
        y_d = nc.dram_tensor("y_d", [NP, D], F32)
        part_d = nc.dram_tensor("part_d", [NG, P, TG * D], F32)
        agg1_g = agg1_d.ap().rearrange("(g p j) w -> g p (j w)", p=P, j=TG)
        agg2_g = agg2_d.ap().rearrange("(g p j) w -> g p (j w)", p=P, j=TG)
        y_g = y_d.ap().rearrange("(g p j) w -> g p (j w)", p=P, j=TG)
        x_g = x.rearrange("(g p j) w -> g p (j w)", p=P, j=TG)
        out_g = out.rearrange("(g p j) w -> g p (j w)", p=P, j=TG)
        src_g = src.rearrange("(g p j) -> g p j", p=P, j=TG)
        dst_g = dst.rearrange("(g p j) -> g p j", p=P, j=TG)
        dst_row = dst.rearrange("(g a e) -> g a e", a=1, e=GROUP)

        bank = [ctx.enter_context(nc.psum_tensor(f"bank{i}", [P, D], F32)) for i in range(8)]

        ident = sb("ident", [P, P])
        tri = sb("tri", [P, P])
        bmask = sb("bmask", [P, P])
        valid = sb("valid", [P, 4], F32R)
        trash = sb("trash", [P, 1])
        iota8 = sb("iota8", [P, EXP])
        b1c = sb("b1c", [P, KC])
        fb1c = sb("fb1c", [P, KC])
        brc = sb("brc", [EXP, 1])
        bias = sb("bias", [P, D])
        KS = sb("KS", [P, KC, P])
        ksum = sb("ksum", [P, KC])
        rdeg = sb("rdeg", [P, NT])

        arena = sb("arena", [P, SLOTS, TG * D])
        base = nc.sbuf_base - SLOTS * TG * D * 4

        def at(name, first, count, dt=F32, shape=None):
            return nc.alloc_sbuf_tensor_at(name, shape or [P, count, TG, D], dt,
                                           offset=base + int(first * TG * D * 4))

        def halves(name, first, count=1):
            return [at(f"{name}_high", first, count, F32R), at(f"{name}_low", first + count, count, F32R)]

        wkTs, wqTs = at("wkTs", 13, 1), at("wqTs", 14, 1)
        blockP = at("blockP", 17, 1, shape=[P, KC, P])
        wqs = halves("wq_made", 15)
        ax, axn = at("a_x", 0, 2), at("a_xn", 6, 1)
        xT = halves("xnT", 2, 2)
        axr, aph = halves("a_xn_rows", 7), halves("a_phi", 9)
        Wk = halves("Wk", 11)
        W1r, W1l, W2l = halves("W1r", 13), halves("W1l", 15), halves("W2l", 17)
        raw = at("raw_weight", 19, 1)
        spare = [at("spare_high", 20, 1, F32R), at("spare_low", 19, 1, F32R)]
        wvs, wps = at("wvs", 19, 1), at("wps", 20, 1)
        krow = at("key_sums", 1.5, 1, shape=[2, D])
        K2T, kvT = at("K2T", 0, 1), at("kvT", 1, 1, shape=[P, KC, P])
        Mf = halves("M_made", 8)
        by, baT, bhT = at("b_y", 0, 2), halves("aggT", 6), halves("hT_made", 8)
        bagg = at("b_agg", 10, 3, shape=[P, 2, TG, AW])
        Wq = halves("Wq", 19)
        mx_, mhT, mqz = at("m_x", 0, 2), halves("hT", 6, 2), halves("qz", 10, 2)
        M, W2r = halves("M", 15), halves("W2r", 17)
        fx, fxT, frelu, fhm = at("f_x2", 0, 4), halves("x2T", 4, 2), at("f_relu", 8, 1), halves("masked", 9)
        F1, F2 = halves("F1", 11), halves("F2", 13)
        maskT, fa = at("maskT", 15, 1, F32R, [EXP, 2, GROUP]), at("f_xn", 16, 2)
        fb2s = at("fb2_halves", 18, 1, F32R, [EXP, 2, D])
        expand = at("expand", 18.5, 1, F32R, [EXP, KC, P])
        wrs = at("wr_halves", 19, 1, F32R, [P, 2, KC, EXP])
        lgT = at("logitsT", 19.5, 1, shape=[EXP, GROUP])
        craw = at("ffn_raw", 20, 1, shape=[P, 4, D])

        def router(name, place, cols, dt=F32):
            return nc.alloc_sbuf_tensor_at(name, [P, TG, cols], dt,
                                           offset=base + (19 * TG * D + 256 + place * TG * EXP) * 4)

        lg, mx, ix, onehot = (router("logit", 0, EXP), router("mx", 1, 8), router("ix", 2, 8, U32),
                              router("onehot", 3, EXP))
        ixf, topd, tope, gate, rtop = (router(n, 4 + i, 1) for i, n in
                                       enumerate(("ixf", "topd", "tope", "gate", "rtop")))

        esrc = sb("esrc", [P, 2, TG], I32)
        edst = sb("edst", [P, 2, TG], I32)
        erow = sb("erow", [P, 2, GROUP], I32)
        dstf = sb("dstf", [P, 2, TG])
        todump = sb("todump", [P, 2, TG])
        G = sb("G", [P, 4, D])
        S = sb("S", [P, 4, P])
        Sj = sb("Sj", [P, P])
        cnt = sb("cnt", [P, 4])
        cnt1 = sb("cnt1", [P, 4])
        eidx = sb("eidx", [P, 4, 1], I32)
        O = sb("O", [P, 4, AW])
        est = sb("est", [P, 6])

        st = sb("st", [P, 6])
        mv = sb("mv", [P, TG, 2])
        veps = sb("veps", [P, TG])
        rs = sb("rs", [P, TG])
        nhalf = sb("nhalf", [P, TG])
        low = sb("low", [P, 4, D])
        rd = sb("rd", [P, 2, TG])
        pd = sb("pd", [P, D])


        s_w = sem("weights_in")
        s_zero, s_valid, s_hi = sem("zero_ready"), sem("valid_in"), sem("weight_high")
        s_f = sem("expert_weights_in")
        s_raw, s_split, s_kept = sem("raw_weight_in"), sem("weight_split"), sem("split_weight_stored")
        s_wk, s_late, s_fw = sem("qk_weights_in"), sem("late_constants_in"), sem("fold_weights_in")
        s_wqst, s_mst, s_wq = sem("wq_stored"), sem("m_stored"), sem("wq_in")
        s_w2r, s_m, s_craw, s_csp = sem("w2r_in"), sem("m_in"), sem("ffn_raw_in"), sem("ffn_raw_split")
        s_z = sem("zeroed")
        s_foldc = sem("fold_copied")
        s_prep = sem("prepared")
        s_phase = sem("phase_done")

        def phase_end(eng, k):
            eng.drain().then_inc(s_phase, 1)
            eng.wait_ge(s_phase, 5 * k)

        zero = sb("zero", [P, AW // 4])

        def clear(eng, agg_g, g, width, cleared):
            eng.dma_start(agg_g[g].rearrange("p (q w) -> p q w", w=width // 4),
                          zero[:, None, 0:width // 4].to_broadcast([P, 4 * TG, width // 4])
                          ).then_inc(cleared, 16)

        s_past = {}

        def need_apart(eng, sem, value):
            need(eng, sem, value)
            if not isinstance(value, int):
                eng.sem_inc(s_past[eng.engine], 1)

        e_in = [sem(f"edge_lists_in{b}") for b in range(2)]
        e_f = sem("edge_targets_float")
        e_td = sem("edge_trash_offset")
        e_g = [sem(f"edge_gathered{i}") for i in range(4)]
        e_cnt, e_cnt1, e_ix = sem("edge_repeats"), sem("edge_repeated"), sem("edge_rows")
        e_st = sem("edge_stats")
        e_s = sem("edge_tile_ready")
        e_mm = sem("edge_summed")
        e_o = sem("edge_sums_out")
        e_sc = sem("edge_scattered")
        s_z1, s_z2 = sem("agg1_cleared"), sem("agg2_cleared")

        def flat(buf, b):
            return buf[:, b].rearrange("p c n -> p (c n)").bitcast(F32)

        def low_half(eng, out_, full, high):
            return eng.tensor_tensor(out_, full, high.bitcast(F32), ALU.subtract)

        def pair(name):
            return [sem(f"{name}{b}") for b in range(2)]

        a_x, a_st = pair("keys_x_in"), pair("keys_xnT_stored")
        a_s1, a_s2, a_s3 = sem("keys_stats"), sem("keys_mean_var"), sem("keys_rstd")
        a_ve, f_ve = sem("keys_var_eps"), sem("ffn_var_eps")
        a_xn, a_tr, a_ev = sem("keys_xn"), sem("keys_transposed"), sem("keys_xnT")
        a_kp, a_min, a_exp = sem("keys_k"), sem("keys_min"), sem("keys_exp")
        a_phi, a_T = sem("keys_phi"), sem("keys_summed")
        a_xh, a_xl = sem("keys_xn_high"), sem("keys_xn_low")
        a_tl, a_ph, a_pl = sem("keys_xnT_low"), sem("keys_phi_high"), sem("keys_phi_low")
        k_pe = sem("weights_folded")
        k_hi, k_lo = sem("folded_high"), sem("folded_low")
        c_mh, c_ml = sem("fold_m_high"), sem("fold_m_low")
        b_al, b_hh, b_hl = sem("hid_aggT_low"), sem("hid_h_high"), sem("hid_h_low")
        m_qh, m_ql = sem("mix_qz_high"), sem("mix_qz_low")
        f_tl, f_hh, f_hl = sem("ffn_xnT_low"), sem("ffn_masked_high"), sem("ffn_masked_low")
        c_kr = sem("fold_key_sums_turned")
        c_k2, c_kv, c_kvc, c_m = sem("fold_k2"), sem("fold_kv"), sem("fold_kv_kept"), sem("fold_m")
        b_xt, b_agg, b_yst = (pair(n) for n in ("hid_xnT_in", "hid_agg_in", "hid_y_stored"))
        b_hst = sem("hid_h_stored")
        b_d, b_r, b_ag = sem("hid_degree"), sem("hid_rdegree"), sem("hid_mean")
        b_tr, b_ev, b_h, b_th = sem("hid_transposed"), sem("hid_aggT"), sem("hid_h"), sem("hid_tanh")
        b_y, b_yo = sem("hid_y"), sem("hid_y_out")
        m_xt, m_ht, m_x, m_st = (pair(n) for n in ("mix_xnT_in", "mix_hT_in", "mix_x_in",
                                                   "mix_stored"))
        m_q, m_min, m_exp, m_phi = sem("mix_q"), sem("mix_min"), sem("mix_exp"), sem("mix_phi")
        m_den, m_z, m_qz, m_xb = sem("mix_den"), sem("mix_z"), sem("mix_qz"), sem("mix_x_bias")
        m_p, m_po = sem("mix_product"), sem("mix_part")
        f_p, f_st = ([sem(f"{n}{k}") for k in range(4)] for n in ("ffn_part_in", "ffn_stored"))
        f_a, f_lt = pair("ffn_agg_in"), sem("ffn_logits_turned")
        f_rd, f_x2 = sem("ffn_rdegree"), sem("ffn_x2")
        f_s1, f_s2, f_s3 = sem("ffn_stats"), sem("ffn_mean_var"), sem("ffn_rstd")
        f_xn, f_tr, f_ev, f_r = sem("ffn_xn"), sem("ffn_transposed"), sem("ffn_xnT"), sem("ffn_logits")
        f_l, f_mx, f_ix, f_ixf = sem("ffn_logits_b"), sem("ffn_max"), sem("ffn_index"), sem("ffn_indexf")
        f_d, f_e, f_g, f_oh = sem("ffn_top"), sem("ffn_top_exp"), sem("ffn_gate"), sem("ffn_onehot")
        f_rt, f_lg = sem("ffn_top_reciprocal"), sem("ffn_logits_kept")
        f_mt, f_mtc, f_h1, f_re = sem("ffn_maskT"), sem("ffn_maskT_kept"), sem("ffn_h"), sem("ffn_relu")
        f_m, f_hm, f_h2, f_out = sem("ffn_mask"), sem("ffn_masked"), sem("ffn_product"), sem("ffn_out")

        for e in (nc.vector, nc.gpsimd, nc.tensor):
            s_past[e.engine] = sem(f"wait_passed_{len(s_past)}")

        block = ctx.enter_context(nc.Block())

        def edge_load(sp, ph, turn, b):
            g = 2 * turn + b
            need(sp, e_s, ph * NT + 4 * g - 4)
            for to, of in ((esrc[:, b, :], src_g[g]), (edst[:, b, :], dst_g[g]),
                           (erow[:, b, :], dst_row[g].to_broadcast([P, GROUP]))):
                sp.dma_start(to, of).then_inc(e_in[b], 16)

        def edge_gather(pool, ph, turn, k, table):
            t = 8 * turn + k
            if active(t, 0, NT):
                b, j = k // 4, k % 4
                if j == 0:
                    need_apart(pool, e_in[b], 48 * (ph * PAIRS + turn + 1))
                need_apart(pool, e_mm, ph * NT + t - 3)
                pool.indirect_dma_start(G[:, j, :], None, table,
                                        bass.IndirectOffsetOnAxis(ap=esrc[:, b, j:j + 1], axis=0)
                                        ).then_inc(e_g[j], 16)

        def edge_scatter(pool, ph, turn, k, agg, width):
            t = 8 * turn + k
            if active(t, 4, NT):
                j = (k - 4) % 4
                need_apart(pool, e_o, ph * NT + t - 3)
                need_apart(pool, e_sc, 16 * (ph * NT + t - 4))
                pool.indirect_dma_start(agg, bass.IndirectOffsetOnAxis(ap=eidx[:, j, 0:1], axis=0),
                                        O[:, j, 0:width], None, compute_op=ALU.add).then_inc(e_sc, 16)

        def edge_dve(dve, ph, turn, k, norm):
            t = 8 * turn + k
            if not active(t, 2, NT):
                return
            turn1, kk = lagged(turn, k, 2)
            b, j = kk // 4, kk % 4
            u, ug = ph * NT + t - 1, ph * NG + 2 * turn1 + b
            if j == 0:
                dve.wait_ge(e_in[b], 48 * (ph * PAIRS + turn1 + 1))
                dve.tensor_copy(dstf[:, b, :], edst[:, b, :]).then_inc(e_f, 1)
                dve.wait_ge(e_f, ug + 1)
                dve.tensor_scalar(todump[:, b, :], dstf[:, b, :], -1.0, trash[:, 0:1], ALU.mult, ALU.add
                                  ).then_inc(e_td, 1)
            need(dve, e_mm, u - 4)
            need(dve, e_sc, 16 * (u - 4))
            row = erow[:, b, j:GROUP:TG]
            dve.scalar_tensor_tensor(Sj[:, :], row, dstf[:, b, j:j + 1], tri[:, :], ALU.is_equal,
                                     ALU.mult, accum_out=cnt[:, j:j + 1]).then_inc(e_cnt, 1)
            dve.tensor_scalar(S[:, j, :], row, dstf[:, b, j:j + 1], 0.0, ALU.is_equal, ALU.add,
                              accum_out=O[:, j, D:D + 1])
            dve.wait_ge(e_cnt, u)
            dve.tensor_scalar(cnt1[:, j:j + 1], cnt[:, j:j + 1], 1.0, None, ALU.min).then_inc(e_cnt1, 1)
            dve.wait_ge(e_cnt1, u)
            if j == 0:
                dve.wait_ge(e_td, ug + 1)
            if not norm:
                dve.wait_ge(e_g[j], 16 * (NT // 4 + 2 * turn1 + b + 1))
            ix = dve.scalar_tensor_tensor(eidx[:, j, :], cnt1[:, j:j + 1], todump[:, b, j:j + 1],
                                          dstf[:, b, j:j + 1], ALU.mult, ALU.add)
            if not norm:
                ix.then_inc(e_s, 1)

        def edge_pe(pe, ph, turn, k, psum):
            t = 8 * turn + k
            if active(t, 3, NT):
                j = (k - 3) % 4
                pe.wait_ge(e_s, ph * NT + t - 2)
                need(pe, e_o, ph * NT + t - 3)
                pe.matmul(psum, S[:, j, :], G[:, j, :], start=True, stop=True).then_inc(e_mm, 1)

        def edge_act(act, ph, turn, k, psum):
            t = 8 * turn + k
            if active(t, 3, NT):
                j = (k - 3) % 4
                act.wait_ge(e_mm, ph * NT + t - 2)
                need(act, e_sc, 16 * (ph * NT + t - 6))
                act.copy(O[:, j, 0:D], psum).then_inc(e_o, 1)

        s_bp = sem("feature_blocks_in")

        def kpn(w):
            return w.rearrange("(c p) n -> p c n", p=P)

        first = [(wkTs[:, 0], kpn(wkT)), (wqTs[:, 0], kpn(wqT))]
        consts = [(ident[:], ident_in), (tri[:], tri_in), (trash[:], trash_in)]
        late = [(bmask[:], bmask_in), (iota8[:], iota_in), (b1c[:], b1), (fb1c[:], fb1),
                (brc[:], br), (bias[:], b2.to_broadcast([P, D])),
                (pd[:], bproj.to_broadcast([P, D]))]
        splits = [(w1rT, W1r, None), (w1lT, W1l, None), (w2lT, W2l, None),
                  (w2rT, None, w2r_d), (f1, None, f1_d), (f2, None, f2_d)]

        turned = (0, 1, 5, 4)

        raw_at = {2: 1, 3: 2, 4: 3, 5: 4, 6: 5, 8: 6}

        @block.sync
        def _(sp):
            for to, of in first:
                sp.dma_start(to, of).then_inc(s_wk, 16)
            sp.dma_start(low[:, 0, 0:4], valid_in).then_inc(s_valid, 16)
            for to, of in consts:
                sp.dma_start(to, of).then_inc(s_w, 16)
            sp.wait_ge(s_z, 1)
            for h in range(HEADS):
                o = HD * (h % 2)
                sp.dma_start(blockP[o:o + HD, h // 2, o:o + HD], pmat[h]).then_inc(s_bp, 16)
            sp.dma_start(raw[:, 0], kpn(splits[0][0])).then_inc(s_raw, 16)
            for to, of in late:
                sp.dma_start(to, of).then_inc(s_late, 16)
            for b in range(2):
                sp.dma_start(flat(ax, b), x_g[b]).then_inc(a_x[b], 16)
                edge_load(sp, 0, 0, b)
            sp.wait_ge(s_zero, 1)
            for g in range(NG):
                clear(sp, agg1_g, g, AW, s_z1)
            sp.wait_ge(k_lo, 2 * KC)
            for n in range(2):
                sp.dma_start(wq_d[n][:], flat(wqs[n], 0)).then_inc(s_wqst, 16)
            phase_end(sp, 1)

            def keys(turn, b):
                g = 2 * turn + b
                if isinstance(g, int) and g < 2:
                    return
                sp.wait_ge(a_xn, 4 * (g - 1))
                sp.dma_start(flat(ax, b), x_g[g]).then_inc(a_x[b], 16)
                edge_load(sp, 0, turn, b)
                if isinstance(g, int) and g in raw_at:
                    i = raw_at[g]
                    sp.wait_ge(s_split, 4 * i)
                    if splits[i - 1][2] is not None:
                        for n in range(2):
                            sp.dma_start(splits[i - 1][2][n][:], flat(spare[n], 0)).then_inc(s_kept, 16)
                        sp.wait_ge(s_kept, 32 * (i - 3))
                    if i < len(splits):
                        sp.dma_start(raw[:, 0], kpn(splits[i][0])).then_inc(s_raw, 16)
                    else:
                        sp.dma_start(wvs[:, 0], kpn(wv)).then_inc(s_fw, 16)
                        sp.dma_start(wps[:, 0], kpn(wproj)).then_inc(s_fw, 16)
            group_turns(sp, keys, 0, head=5)
            phase_end(sp, 2)

            def hidden(turn, b):
                g = 2 * turn + b
                if active(g, 0, NG):
                    need(sp, b_h, 4 * (g - 1))
                    for n in range(2):
                        sp.dma_start(flat(xT[n], b), xnT_d[n][g]).then_inc(b_xt[b], 16)
                    need(sp, b_tr, 4 * (g - 1))
                    sp.dma_start(bagg[:, b].rearrange("p j w -> p (j w)"), agg1_g[g]).then_inc(b_agg[b], 16)
                if isinstance(g, int) and g == 1:
                    sp.wait_ge(c_ml, KC)
                    for n in range(2):
                        sp.dma_start(m_d[n][:], flat(Mf[n], 0)).then_inc(s_mst, 16)
                    sp.wait_ge(s_mst, 32)
                    for n in range(2):
                        sp.dma_start(flat(Wq[n], 0), wq_d[n][:]).then_inc(s_wq, 16)
                if active(g, 1, NG):
                    sp.wait_ge(b_hl, 4 * g)
                    for n in range(2):
                        sp.dma_start(hT_d[n][g - 1], flat(bhT[n], 0)).then_inc(b_hst, 16)
                    sp.wait_ge(b_yo, 4 * g)
                    sp.dma_start(y_g[g - 1], flat(by, 1 - b)).then_inc(b_yst[1 - b], 16)
            group_turns(sp, hidden, 1)
            for b in range(2):
                sp.wait_ge(b_yst[b], 16 * PAIRS)
            sp.wait_ge(b_hst, 32 * NG)
            phase_end(sp, 3)

            def mix(turn, b):
                g = 2 * turn + b
                if active(g, 0, NG):
                    need(sp, m_q, 4 * (g - 1))
                    for n in range(2):
                        sp.dma_start(flat(xT[n], b), xnT_d[n][g]).then_inc(m_xt[b], 16)
                    edge_load(sp, 1, turn, b)
                if isinstance(g, int) and g == 0:
                    for n in range(2):
                        sp.dma_start(flat(W2r[n], 0), w2r_d[n][:]).then_inc(s_w2r, 16)
                        sp.dma_start(flat(M[n], 0), m_d[n][:]).then_inc(s_m, 16)
                if active(g, 3, NG):
                    sp.wait_ge(m_po, 4 * (g - 2))
                    sp.dma_start(part_d[g - 3], flat(mx_, 1 - b)).then_inc(m_st[1 - b], 16)
                if active(g, 1, NG):
                    turn1, b1_ = lagged(turn, b, 1, 2)
                    need(sp, m_p, 4 * (g - 2))
                    for n in range(2):
                        sp.dma_start(flat(mhT[n], b1_), hT_d[n][g - 1]).then_inc(m_ht[b1_], 16)
                    need(sp, m_st[b1_], 16 * turn1)
                    sp.dma_start(flat(mx_, b1_), x_g[g - 1]).then_inc(m_x[b1_], 16)
            group_turns(sp, mix, 3, head=2)
            for b in range(2):
                sp.wait_ge(m_st[b], 16 * PAIRS)
            phase_end(sp, 4)

            sp.dma_start(craw[:, 0, 0:KC * EXP].rearrange("p (c e) -> p c e", c=KC), kpn(wr)
                         ).then_inc(s_craw, 16)
            sp.dma_start(craw[0:EXP, 1, :], fb2).then_inc(s_craw, 16)
            sp.dma_start(craw[0:EXP, 2, :], expand_in.rearrange("e c p -> e (c p)")).then_inc(s_craw, 16)

            def ffn(turn, k):
                g, b = 4 * turn + k, k % 2
                if active(g, 0, NG):
                    need(sp, f_st[k], 16 * turn)
                    sp.dma_start(flat(fx, k), part_d[g]).then_inc(f_p[k], 16)
                    need(sp, f_tr, 4 * (g - 1))
                    sp.dma_start(flat(fa, b), agg2_g[g]).then_inc(f_a[b], 16)
                if isinstance(g, int) and g == 0:
                    for n in range(2):
                        sp.dma_start(flat(F1[n], 0), f1_d[n][:]).then_inc(s_f, 16)
                        sp.dma_start(flat(F2[n], 0), f2_d[n][:]).then_inc(s_f, 16)
                if active(g, 2, NG):
                    sp.wait_ge(f_out, 4 * (g - 1))
                    sp.dma_start(out_g[g - 2], flat(fx, (k - 2) % 4)).then_inc(f_st[(k - 2) % 4], 16)
            quad_turns(sp, ffn, 2)
            for k in range(4):
                sp.wait_ge(f_st[k], 16 * NG // 4)

        @block.gpsimd
        def _(pool):
            pool.memset(zero[:, :], 0.0).then_inc(s_zero, 1)
            pool.memset(nhalf[:, :], -0.5)
            pool.memset(O[:, :, :], 0.0)
            pool.memset(mv[:, :, :], 1.0)
            pool.wait_ge(s_valid, 16)
            pool.tensor_copy(valid[:, :], low[:, 0, 0:4]).then_inc(s_prep, 1)
            phase_end(pool, 1)

            def split(i, q):
                if q == 0:
                    pool.wait_ge(s_raw, 16 * (i + 1))
                    if i == 1:
                        pool.wait_ge(s_wqst, 32)
                high, lo = (h[:, 0, q, :] for h in splits[i][1] or spare)
                pool.tensor_copy(high, raw[:, 0, q, :]).then_inc(s_hi, 1)
                pool.wait_ge(s_hi, 4 * i + q + 1)
                low_half(pool, lo, raw[:, 0, q, :], high).then_inc(s_split, 1)

            def keys(turn, k):
                t = 8 * turn + k
                if active(t, 0, NT + 2):
                    need_apart(pool, a_s2, t + 1)
                    pool.tensor_scalar(veps[:, 0:2], mv[:, 0:2, 1], EPS, None, ALU.add).then_inc(a_ve, 1)
                    pool.wait_ge(a_ve, t + 1)
                    pool.tensor_tensor(rs[:, 0:2], veps[:, 0:2], nhalf[:, 0:2], ALU.pow).then_inc(a_s3, 1)
                edge_gather(pool, 0, turn, k, x)
                if active(t, 0, NT):
                    pool.wait_ge(a_xh, t + 1)
                    need(pool, a_T, t - 3)
                    low_half(pool, axr[1][:, 0, k % 4, :], axn[:, 0, k % 4, :], axr[0][:, 0, k % 4, :]
                             ).then_inc(a_xl, 1)
                if isinstance(t, int) and t == 4:
                    pool.wait_ge(s_z1, 16 * NG)
                edge_scatter(pool, 0, turn, k, agg1_d.ap(), AW)
                if isinstance(t, int) and t % 5 and t // 5 < len(splits):
                    split(t // 5, t % 5 - 1)
                if isinstance(t, int) and t == 5 * len(splits):
                    pool.wait_ge(s_late, 16 * len(late))
                    pool.tensor_tensor(bias[:, :], bias[:, :], pd[:, :], ALU.add)
            turns(pool, keys, 4, head=4)
            pool.wait_ge(e_sc, 16 * NT)
            phase_end(pool, 2)
            phase_end(pool, 3)
            pool.wait_ge(s_z2, 16 * NG)

            def step(turn, k):
                t = 8 * turn + k
                edge_gather(pool, 1, turn, k, y_d.ap())
                edge_scatter(pool, 1, turn, k, agg2_d.ap(), D)
                if active(t, 7, NT):
                    turn1, kk = lagged(turn, k, 7)
                    b, j = kk // 4, kk % 4
                    if j == 0:
                        pool.wait_ge(m_x[b], 16 * (turn1 + 1))
                    xr = mx_[:, b, j, :]
                    pool.tensor_tensor(xr, xr, bias[:, :], ALU.add).then_inc(m_xb, 1)
            turns(pool, step, 7)
            pool.wait_ge(e_sc, 16 * 2 * NT)
            phase_end(pool, 4)

            def ffn(turn, b):
                for j in range(TG):
                    t = 4 * (2 * turn + b) + j
                    need_apart(pool, f_s2, t + 1)
                    pool.tensor_scalar(veps[:, j:j + 1], mv[:, j, 1:2], EPS, None, ALU.add
                                       ).then_inc(f_ve, 1)
                    pool.wait_ge(f_ve, t + 1)
                    pool.tensor_tensor(rs[:, j:j + 1], veps[:, j:j + 1], nhalf[:, j:j + 1], ALU.pow
                                       ).then_inc(f_s3, 1)
            group_turns(pool, ffn, 0)

        @block.scalar
        def _(act):
            for i in range(2 * KC):
                act.wait_ge(k_pe, i + 1)
                act.copy((Wk if i < KC else wqs)[0][:, 0, i % KC, :], bank[i][:, :]).then_inc(k_hi, 1)
            phase_end(act, 1)

            def keys(turn, k):
                t, b, j = 8 * turn + k, k // 4, k % 4
                if active(t, 0, NT):
                    act.wait_ge(a_xn, t + 1)
                    need(act, a_T, t - 3)
                    act.copy(axr[0][:, 0, j, :], axn[:, 0, j, :]).then_inc(a_xh, 1)
                    act.wait_ge(a_tr, t + 1)
                    if j == 0:
                        need(act, a_kp, t - 4)
                        need(act, a_st[b], 32 * turn)
                    act.copy(xT[0][:, b, :, j * P:(j + 1) * P],
                             bank[5][:, :].rearrange("p (c n) -> p c n", c=KC)).then_inc(a_ev, 1)
                if active(t, 1, NT):
                    act.wait_ge(a_kp, t)
                    need(act, a_pl, t - 4)
                    lo = low[:, (k - 1) % 4, :]
                    act.activation(lo, bank[6][:, :], ACT.Relu, scale=-1.0).then_inc(a_min, 1)
                    act.wait_ge(a_min, t)
                    act.activation(lo, lo, ACT.Exp, scale=-1.0).then_inc(a_exp, 1)
                edge_act(act, 0, turn, k, bank[7][:, :])
                if active(t, 1, NT):
                    act.wait_ge(a_phi, t)
                    need(act, a_T, t - 4)
                    act.copy(aph[0][:, 0, (k - 1) % 4, :], low[:, (k - 1) % 4, :]).then_inc(a_ph, 1)
                if active(t, 0, NT) and j == 3:
                    act.wait_ge(a_tl, t + 1)
                    act.wait_ge(a_ev, t + 1)
                    for n in range(2):
                        act.dma_start(xnT_d[n][2 * turn + b], flat(xT[n], b)).then_inc(a_st[b], 16)
                    clear(act, agg2_g, 2 * turn + b, D, s_z2)
            turns(act, keys, 3)
            for b in range(2):
                act.wait_ge(a_st[b], 32 * PAIRS)
            act.wait_ge(s_z2, 16 * NG)
            phase_end(act, 2)

            act.wait_ge(s_mst, 32)
            def hidden(turn, b):
                g = 2 * turn + b
                for j in range(TG):
                    act.wait_ge(b_tr, 4 * g + j + 1)
                    if j == 0:
                        need(act, b_h, 4 * g)
                    act.copy(baT[0][:, 0, :, j * P:(j + 1) * P],
                             bank[j % 2][:, :].rearrange("p (c n) -> p c n", c=KC)).then_inc(b_ev, 1)
                for o in range(KC):
                    act.wait_ge(b_h, 4 * g + o + 1)
                    need(act, b_hl, 4 * (g - 1) + o + 1)
                    act.activation(low[:, o, :], bank[2 + o % 2][:, :], ACT.Tanh,
                                   bias=b1c[:, o:o + 1]).then_inc(b_th, 1)
                    if o == 0:
                        need(act, b_y, 4 * g)
                        need(act, b_hst, 32 * g)
                    act.wait_ge(b_th, 4 * g + o + 1)
                    act.copy(bhT[0][:, 0, o, :], low[:, o, :]).then_inc(b_hh, 1)
            group_turns(act, hidden, 0)
            phase_end(act, 3)

            def mix(turn, k):
                t = 8 * turn + k
                if active(t, 1, NT):
                    act.wait_ge(m_q, t)
                    need(act, m_ql, t - 4)
                    lo = low[:, (k - 1) % 4, :]
                    act.activation(lo, bank[(k - 1) % 2][:, :], ACT.Relu, scale=-1.0).then_inc(m_min, 1)
                    act.wait_ge(m_min, t)
                    act.activation(lo, lo, ACT.Exp, scale=-1.0).then_inc(m_exp, 1)
                edge_act(act, 1, turn, k, bank[7][:, :])
                if active(t, 3, NT):
                    turn3, kk = lagged(turn, k, 3)
                    act.wait_ge(m_qz, t - 2)
                    need(act, m_p, 4 * (2 * turn3 + kk // 4 - 1))
                    act.copy(mqz[0][:, kk // 4, kk % 4, :], low[:, kk % 4, :]).then_inc(m_qh, 1)
            turns(act, mix, 3, head=2)
            phase_end(act, 4)

            act.wait_ge(s_craw, 48)
            act.copy(wrs[:, 0].rearrange("p c e -> p (c e)"), craw[:, 0, 0:KC * EXP]).then_inc(s_csp, 1)
            act.copy(fb2s[:, 0, :], craw[0:EXP, 1, :]).then_inc(s_csp, 1)
            act.copy(expand[:, :, :].rearrange("e c p -> e (c p)"), craw[0:EXP, 2, :]).then_inc(s_csp, 1)

            def ffn(turn, k):
                g, b = 4 * turn + k, k % 2
                if active(g, 1, NG):
                    for c in range(KC):
                        act.wait_ge(f_h1, 4 * (g - 1) + c + 1)
                        need(act, f_hl, 4 * (g - 2) + c + 1)
                        act.activation(frelu[:, 0, c, :], bank[2 + c % 2][:, :], ACT.Relu,
                                       bias=fb1c[:, c:c + 1]).then_inc(f_re, 1)
                        act.wait_ge(f_hm, 4 * (g - 1) + c + 1)
                        if c == 0:
                            need(act, f_h2, 4 * (g - 1))
                        act.copy(fhm[0][:, 0, c, :], frelu[:, 0, c, :]).then_inc(f_hh, 1)
                if active(g, 0, NG):
                    for j in range(TG):
                        act.wait_ge(f_tr, 4 * g + j + 1)
                        if j == 0:
                            need(act, f_h1, 4 * (g - 1))
                        act.copy(fxT[0][:, b, :, j * P:(j + 1) * P],
                                 bank[turned[j]][:, :].rearrange("p (c n) -> p c n", c=KC)
                                 ).then_inc(f_ev, 1)
                    act.wait_ge(f_r, g + 1)
                    need(act, f_lt, g)
                    act.activation(lgT[:, :], bank[5][0:EXP, :], ACT.Identity, bias=brc[:, 0:1]
                                   ).then_inc(f_l, 1)
                    act.wait_ge(f_d, g + 1)
                    act.activation(tope[:, :, 0], topd[:, :, 0], ACT.Exp).then_inc(f_e, 1)
                    act.wait_ge(f_mt, g + 1)
                    act.copy(maskT[:, b, :], bank[5][0:EXP, :]).then_inc(f_mtc, 1)
            quad_turns(act, ffn, 1)

        @block.vector
        def _(dve):
            dve.memset(blockP[:, :, :], 0.0).then_inc(s_z, 1)
            for i in range(2 * KC):
                dve.wait_ge(k_hi, i + 1)
                w = Wk if i < KC else wqs
                low_half(dve, w[1][:, 0, i % KC, :], bank[i][:, :], w[0][:, 0, i % KC, :]).then_inc(k_lo, 1)
            phase_end(dve, 1)

            dve.wait_ge(s_w, 16 * len(consts))
            def keys(turn, k):
                t, b, j = 8 * turn + k, k // 4, k % 4
                if active(t, 0, NT):
                    if j == 0:
                        dve.wait_ge(a_x[b], 16 * (turn + 1))
                    xr = ax[:, b, j, :]
                    dve.bn_stats(st[:, :], xr).then_inc(a_s1, 1)
                if active(t, 2, NT):
                    turn2, kk = lagged(turn, k, 2)
                    dve.wait_ge(e_g[kk % 4], 16 * (2 * turn2 + kk // 4 + 1))
                    dve.bn_stats(est[:, :], G[:, kk % 4, :]).then_inc(e_st, 1)
                if active(t, 0, NT):
                    need_apart(dve, a_s1, t + 1)
                    last = dve.bn_aggr(mv[:, 0, :], st[:, :])
                if active(t, 2, NT):
                    need_apart(dve, e_st, t - 1)
                    last = dve.bn_aggr(mv[:, 1, :], est[:, :])
                if active(t, 0, NT + 2):
                    last.then_inc(a_s2, 1)
                edge_dve(dve, 0, turn, k, True)
                if active(t, 2, NT):
                    jj = (k - 2) % 4
                    dve.wait_ge(a_ph, t - 1)
                    need(dve, a_T, t - 5)
                    low_half(dve, aph[1][:, 0, jj, :], low[:, jj, :], aph[0][:, 0, jj, :]).then_inc(a_pl, 1)
                if active(t, 0, NT):
                    dve.wait_ge(a_s3, t + 1)
                    need(dve, a_tr, t - 3)
                    need(dve, a_xl, t - 3)
                    dve.tensor_scalar(axn[:, 0, j, :], xr, mv[:, 0, 0:1], rs[:, 0:1],
                                      ALU.subtract, ALU.mult).then_inc(a_xn, 1)
                if active(t, 2, NT):
                    dve.wait_ge(a_s3, t + 1)
                    Gj = G[:, (k - 2) % 4, :]
                    dve.tensor_scalar(Gj, Gj, mv[:, 1, 0:1], rs[:, 1:2], ALU.subtract, ALU.mult
                                      ).then_inc(e_s, 1)
                if active(t, 0, NT):
                    dve.wait_ge(a_ev, t + 1)
                    low_half(dve, xT[1][:, b, :, j * P:(j + 1) * P],
                             bank[5][:, :].rearrange("p (c n) -> p c n", c=KC),
                             xT[0][:, b, :, j * P:(j + 1) * P]).then_inc(a_tl, 1)
                if active(t, 1, NT):
                    lo = low[:, (k - 1) % 4, :]
                    dve.wait_ge(a_exp, t)
                    dve.scalar_tensor_tensor(lo, bank[6][:, :], 0.0, lo, ALU.max, ALU.add).then_inc(a_phi, 1)
            turns(dve, keys, 2)
            phase_end(dve, 2)

            for i in range(KC):
                dve.tensor_copy(K2T[:, 0, i, :], bank[i][:, :]).then_inc(c_k2, 1)
            dve.tensor_copy(krow[:, :], bank[4][0:2, :]).then_inc(c_k2, 1)
            dve.wait_ge(c_kr, 1)
            dve.tensor_copy(ksum[:, :], bank[5][:, 0:2 * KC:2]).then_inc(c_k2, 1)
            dve.wait_ge(c_k2, KC + 2)
            for c in range(KC):
                dve.tensor_scalar(KS[:, c, :], bmask[:, :], ksum[:, c:c + 1], None, ALU.mult)
            for c in range(KC):
                dve.wait_ge(c_kv, c + 1)
                dve.tensor_tensor(kvT[:, c, :], bank[4 + c][:, 0:P], bmask[:, :], ALU.mult
                                  ).then_inc(c_kvc, 1)
            for c in range(KC):
                dve.wait_ge(c_m, c + 1)
                dve.tensor_copy(Mf[0][:, 0, c, :], bank[c][:, :]).then_inc(c_mh, 1)
                dve.wait_ge(c_mh, c + 1)
                low_half(dve, Mf[1][:, 0, c, :], bank[c][:, :], Mf[0][:, 0, c, :]).then_inc(c_ml, 1)
            dve.wait_ge(s_mst, 32)

            def hidden(turn, b):
                g = 2 * turn + b
                if active(g, 1, NG):
                    for j in range(TG):
                        dve.wait_ge(b_ev, 4 * (g - 1) + j + 1)
                        cols = slice(j * P, (j + 1) * P)
                        low_half(dve, baT[1][:, 0, :, cols],
                                 bank[j % 2][:, :].rearrange("p (c n) -> p c n", c=KC),
                                 baT[0][:, 0, :, cols]).then_inc(b_al, 1)
                if active(g, 2, NG):
                    need(dve, b_yst[b], 16 * (turn - 1))
                    for j in range(TG):
                        dve.wait_ge(b_y, 4 * (g - 2) + j + 1)
                        dve.tensor_copy(by[:, b, j, :], bank[4 + j % 2][:, :]).then_inc(b_yo, 1)
                if active(g, 0, NG):
                    agg = bagg[:, b]
                    dve.wait_ge(b_agg[b], 16 * (turn + 1))
                    dve.tensor_scalar(rd[:, b, :], agg[:, :, D], 1.0, None, ALU.max).then_inc(b_d, 1)
                    dve.wait_ge(b_d, g + 1)
                    dve.reciprocal(rd[:, b, :], rd[:, b, :]).then_inc(b_r, 1)
                    dve.wait_ge(b_r, g + 1)
                    dve.tensor_copy(rdeg[:, bass.ds(4 * g, TG)], rd[:, b, :])
                    for j in range(TG):
                        dve.tensor_scalar(agg[:, j, 0:D], agg[:, j, 0:D], rd[:, b, j:j + 1], None,
                                          ALU.mult).then_inc(b_ag, 1)
                if active(g, 1, NG):
                    for o in range(KC):
                        dve.wait_ge(b_hh, 4 * (g - 1) + o + 1)
                        low_half(dve, bhT[1][:, 0, o, :], low[:, o, :], bhT[0][:, 0, o, :]).then_inc(b_hl, 1)
            group_turns(dve, hidden, 2, head=2)
            phase_end(dve, 3)

            def mix(turn, k):
                t = 8 * turn + k
                if active(t, 4, NT):
                    kk = (k - 4) % 8
                    dve.wait_ge(m_qh, t - 3)
                    low_half(dve, mqz[1][:, kk // 4, kk % 4, :], low[:, kk % 4, :],
                             mqz[0][:, kk // 4, kk % 4, :]).then_inc(m_ql, 1)
                if active(t, 3, NT):
                    dve.wait_ge(m_den, t - 2)
                    need(dve, m_qz, t - 3)
                    dve.reciprocal(pd[:, :], bank[2][:, :]).then_inc(m_z, 1)
                    dve.wait_ge(m_z, t - 2)
                    lz = low[:, (k - 3) % 4, :]
                    dve.tensor_tensor(lz, lz, pd[:, :], ALU.mult).then_inc(m_qz, 1)
                if active(t, 1, NT):
                    lo, pq = low[:, (k - 1) % 4, :], bank[(k - 1) % 2][:, :]
                    dve.wait_ge(m_exp, t)
                    dve.scalar_tensor_tensor(lo, pq, 0.0, lo, ALU.max, ALU.add).then_inc(m_phi, 1)
                edge_dve(dve, 1, turn, k, False)
                if active(t, 9, NT):
                    turn1, kk = lagged(turn, k, 9)
                    xr = mx_[:, kk // 4, kk % 4, :]
                    dve.wait_ge(m_p, t - 8)
                    dve.wait_ge(m_xb, t - 8)
                    dve.tensor_tensor(xr, bank[4 + kk % 2][:, :], xr, ALU.add).then_inc(m_po, 1)
            turns(dve, mix, 9, head=2)
            phase_end(dve, 4)

            dve.wait_ge(s_csp, 3)
            low_half(dve, wrs[:, 1].rearrange("p c e -> p (c e)"), craw[:, 0, 0:KC * EXP],
                     wrs[:, 0].rearrange("p c e -> p (c e)")).then_inc(s_csp, 1)
            low_half(dve, fb2s[:, 1, :], craw[0:EXP, 1, :], fb2s[:, 0, :]).then_inc(s_csp, 1)

            def pre(turn, k, j):
                g, b = 4 * turn + k, k % 2
                if not active(g, 0, NG):
                    return
                x2, xn = fx[:, k, j, :], fa[:, b, j, :]
                t = 4 * g + j
                if j == 0:
                    dve.wait_ge(f_p[k], 16 * (turn + 1))
                    dve.wait_ge(f_a[b], 16 * (2 * turn + k // 2 + 1))
                    dve.tensor_copy(rd[:, b, :], rdeg[:, bass.ds(4 * g, TG)]).then_inc(f_rd, 1)
                    dve.wait_ge(f_rd, g + 1)
                dve.scalar_tensor_tensor(x2, xn, rd[:, b, j:j + 1], x2, ALU.mult, ALU.add
                                         ).then_inc(f_x2, 1)
                dve.wait_ge(f_x2, t + 1)
                dve.bn_stats(st[:, :], x2).then_inc(f_s1, 1)
                need_apart(dve, f_s1, t + 1)
                dve.bn_aggr(mv[:, j, :], st[:, :]).then_inc(f_s2, 1)

            for j in range(TG):
                pre(0, 0, j)

            def ffn(turn, k):
                g, b, k1 = 4 * turn + k, k % 2, (k - 1) % 4

                def out_tile(j):
                    dve.wait_ge(f_h2, 4 * (g - 1) + j + 1)
                    x2 = fx[:, k1, j, :]
                    dve.tensor_tensor(x2, bank[6 + j % 2][:, :], x2, ALU.add).then_inc(f_out, 1)

                for c in range(KC):
                    if active(g, 1, NG):
                        dve.wait_ge(f_re, 4 * (g - 1) + c + 1)
                        dve.wait_ge(f_m, 4 * (g - 1) + c + 1)
                        hm = frelu[:, 0, c, :]
                        dve.tensor_tensor(hm, hm, bank[4][:, :], ALU.mult).then_inc(f_hm, 1)
                        dve.wait_ge(f_hh, 4 * (g - 1) + c + 1)
                        low_half(dve, fhm[1][:, 0, c, :], frelu[:, 0, c, :], fhm[0][:, 0, c, :]
                                 ).then_inc(f_hl, 1)
                    if active(g, 0, NG):
                        dve.wait_ge(f_s3, 4 * g + c + 1)
                        dve.tensor_scalar(fa[:, b, c, :], fx[:, k, c, :], mv[:, c, 0:1],
                                          rs[:, c:c + 1], ALU.subtract, ALU.mult).then_inc(f_xn, 1)
                if active(g, 0, NG):
                    for j in range(TG):
                        cols = slice(j * P, (j + 1) * P)
                        dve.wait_ge(f_ev, 4 * g + j + 1)
                        low_half(dve, fxT[1][:, b, :, cols],
                                 bank[turned[j]][:, :].rearrange("p (c n) -> p c n", c=KC),
                                 fxT[0][:, b, :, cols]).then_inc(f_tl, 1)
                def ahead(j):
                    pre(turn + (k + 1) // 4, (k + 1) % 4, j)

                if active(g, 1, NG):
                    out_tile(0)
                ahead(0)
                ahead(1)
                if active(g, 0, NG):
                    dve.wait_ge(f_lt, g + 1)
                    dve.tensor_copy(lg[:, :, :].rearrange("p j e -> p (j e)"), bank[4][:, 0:TG * EXP]
                                    ).then_inc(f_lg, 1)
                    need_apart(dve, f_lg, g + 1)
                    for j in range(TG):
                        ins = dve.max(mx[:, j, :], lg[:, j, :])
                    ins.then_inc(f_mx, 1)
                    dve.wait_ge(f_mx, g + 1)
                    dve.tensor_tensor(topd[:, :, 0], mx[:, :, 0], mx[:, :, 0], ALU.subtract).then_inc(f_d, 1)
                    for j in range(TG):
                        ins = dve.max_index(ix[:, j, :], mx[:, j, :], lg[:, j, :])
                    ins.then_inc(f_ix, 1)
                    dve.wait_ge(f_ix, g + 1)
                    dve.tensor_copy(ixf[:, :, 0], ix[:, :, 0]).then_inc(f_ixf, 1)
                    dve.wait_ge(f_e, g + 1)
                    dve.reciprocal(rtop[:, :, 0], tope[:, :, 0]).then_inc(f_rt, 1)
                    dve.wait_ge(f_rt, g + 1)
                    dve.tensor_tensor(gate[:, :, 0], tope[:, :, 0], rtop[:, :, 0], ALU.mult).then_inc(f_g, 1)
                    dve.wait_ge(f_g, g + 1)
                    dve.wait_ge(f_ixf, g + 1)
                    for j in range(TG):
                        ins = dve.tensor_scalar(onehot[:, j, :], iota8[:, :], ixf[:, j, :],
                                                gate[:, j, :], ALU.is_equal, ALU.mult)
                    ins.then_inc(f_oh, 1)
                if active(g, 1, NG):
                    out_tile(1)
                ahead(2)
                if active(g, 1, NG):
                    out_tile(2)
                ahead(3)
                if active(g, 1, NG):
                    out_tile(3)
            quad_turns(dve, ffn, 1, last=1)

        @block.tensor
        def _(pe):
            pe.wait_ge(s_wk, 16 * len(first))
            pe.wait_ge(s_bp, 16 * HEADS)
            for i in range(2 * KC):
                w = wkTs if i < KC else wqTs
                for c in range(KC):
                    last = pe.matmul(bank[i][:, c * P:(c + 1) * P], w[:, 0, c, (i % KC) * P:(i % KC + 1) * P],
                                     blockP[:, c, :], start=True, stop=True)
                last.then_inc(k_pe, 1)
            phase_end(pe, 1)
            pe.wait_ge(s_w, 16 * len(consts))

            THREE = ((0, 0), (0, 1), (1, 0))

            def product(out_, lhs, rhs, start=True, stop=True):
                for c in range(KC):
                    for i, (l, r) in enumerate(THREE):
                        last = pe.matmul(out_, lhs(l, c), rhs(r, c), start=start and c == 0 and i == 0,
                                         stop=stop and c == KC - 1 and i == 2)
                return last

            def turn_tile(psum, row):
                for c in range(KC):
                    last = pe.transpose(psum[:, c * P:(c + 1) * P], row[:, c * P:(c + 1) * P], ident[:, :])
                return last

            def keys(turn, k):
                t, b, j = 8 * turn + k, k // 4, k % 4
                if active(t, 0, NT):
                    pe.wait_ge(a_xn, t + 1)
                    need(pe, a_tl, t)
                    turn_tile(bank[5], axn[:, 0, j, :]).then_inc(a_tr, 1)
                edge_pe(pe, 0, turn, k, bank[7][:, :])
                if active(t, 3, NT):
                    turn3, kk = lagged(turn, k, 3)
                    first = isinstance(t, int) and t == 3
                    final = isinstance(t, int) and t == NT + 2
                    pe.wait_ge(a_xl, t - 2)
                    pe.wait_ge(a_pl, t - 2)
                    for c in range(KC):
                        for i, (l, r) in enumerate(THREE):
                            pe.matmul(bank[c][:, :], axr[l][:, 0, kk % 4, c * P:(c + 1) * P],
                                      aph[r][:, 0, kk % 4, :], start=first and i == 0,
                                      stop=final and i == 2, skip_group_check=True)
                    cols = slice(2, 4) if isinstance(t, int) and t - 3 >= NT - TG else slice(0, 2)
                    for n in range(2):
                        last = pe.matmul(bank[4][0:2, :], valid[:, cols],
                                         aph[n][:, 0, kk % 4, :], start=first and n == 0,
                                         stop=final and n == 1, skip_group_check=True)
                    last.then_inc(a_T, 1)
                if active(t, 0, NT):
                    pe.wait_ge(a_tl, t + 1)
                    need(pe, a_phi, t)
                    product(bank[6][:, :], lambda n, c: xT[n][:, b, c, j * P:(j + 1) * P],
                            lambda n, c: Wk[n][:, 0, c, :]).then_inc(a_kp, 1)
            turns(pe, keys, 3, last=1)
            phase_end(pe, 2)

            pe.wait_ge(c_k2, KC + 1)
            for c in range(KC):
                last = pe.transpose(bank[5][:, 2 * c:2 * c + 2], krow[:, c * P:(c + 1) * P], ident[0:2, 0:2])
            last.then_inc(c_kr, 1)
            pe.wait_ge(c_k2, KC + 2)
            pe.wait_ge(s_fw, 32)
            for c in range(KC):
                for i in range(KC):
                    last = pe.matmul(bank[4 + c][:, 0:P], wvs[:, 0, i, c * P:(c + 1) * P],
                                     K2T[:, 0, i, c * P:(c + 1) * P], start=i == 0, stop=i == KC - 1)
                last.then_inc(c_kv, 1)
            for c in range(KC):
                pe.wait_ge(c_kvc, c + 1)
                pe.matmul(bank[c][:, :], kvT[:, c, :], wps[:, 0, c, :], start=True, stop=True
                          ).then_inc(c_m, 1)
            pe.wait_ge(c_ml, KC)

            def hidden(turn, b):
                g = 2 * turn + b
                if active(g, 0, NG):
                    for j in range(TG):
                        pe.wait_ge(b_ag, 4 * g + j + 1)
                        need(pe, b_al, 4 * g + j - 1)
                        turn_tile(bank[j % 2], bagg[:, b, j, 0:D]).then_inc(b_tr, 1)
                if active(g, 1, NG):
                    pe.wait_ge(b_hl, 4 * g)
                    for j in range(TG):
                        need(pe, b_yo, 4 * (g - 1) + j - 1)
                        product(bank[4 + j % 2][:, :], lambda n, c: bhT[n][:, 0, c, j * P:(j + 1) * P],
                                lambda n, c: W2l[n][:, 0, c, :]).then_inc(b_y, 1)
                if active(g, 0, NG):
                    pe.wait_ge(b_xt[b], 32 * (turn + 1))
                    for o in range(KC):
                        need(pe, b_th, 4 * g + o - 1)
                        ph = bank[2 + o % 2][:, :]
                        product(ph, lambda n, c: W1r[n][:, 0, c, o * P:(o + 1) * P],
                                lambda n, c: xT[n][:, b, c, :], stop=False)
                        if o == 0:
                            pe.wait_ge(b_al, 4 * (g + 1))
                        product(ph, lambda n, c: W1l[n][:, 0, c, o * P:(o + 1) * P],
                                lambda n, c: baT[n][:, 0, c, :], start=False).then_inc(b_h, 1)
            group_turns(pe, hidden, 1)
            phase_end(pe, 3)

            pe.wait_ge(s_wq, 32)

            def mix(turn, k):
                t, b, j = 8 * turn + k, k // 4, k % 4
                if active(t, 0, NT):
                    if j == 0:
                        pe.wait_ge(m_xt[b], 32 * (turn + 1))
                    need(pe, m_phi, t - 1)
                    product(bank[j % 2][:, :], lambda n, c: Wq[n][:, 0, c, j * P:(j + 1) * P],
                            lambda n, c: xT[n][:, b, c, :]).then_inc(m_q, 1)
                edge_pe(pe, 1, turn, k, bank[7][:, :])
                if active(t, 8, NT):
                    turn8, kk = lagged(turn, k, 8)
                    b8, j8 = kk // 4, kk % 4
                    if isinstance(t, int) and t == 8:
                        pe.wait_ge(s_w2r, 32)
                        pe.wait_ge(s_m, 32)
                    if j8 == 0:
                        pe.wait_ge(m_ht[b8], 32 * (turn8 + 1))
                        pe.wait_ge(m_ql, t - 8 + 4)
                    need(pe, m_po, t - 9)
                    pp, cols = bank[4 + j8 % 2][:, :], slice(j8 * P, (j8 + 1) * P)
                    product(pp, lambda n, c: mhT[n][:, b8, c, cols], lambda n, c: W2r[n][:, 0, c, :],
                            stop=False)
                    product(pp, lambda n, c: mqz[n][:, b8, c, cols], lambda n, c: M[n][:, 0, c, :],
                            start=False).then_inc(m_p, 1)
                if active(t, 2, NT):
                    j2 = (k - 2) % 4
                    pe.wait_ge(m_phi, t - 1)
                    need(pe, m_z, t - 2)
                    pe.matmul(bank[2][:, :], KS[:, j2, :], low[:, j2, :], start=True, stop=True
                              ).then_inc(m_den, 1)
            turns(pe, mix, 8, head=2)
            phase_end(pe, 4)

            pe.wait_ge(s_csp, 5)
            pe.wait_ge(s_f, 64)

            def ffn(turn, k):
                g, b, b1_ = 4 * turn + k, k % 2, (k - 1) % 2

                def second_layer(j):
                    if not active(g, 1, NG):
                        return
                    need(pe, f_out, 4 * (g - 1) + j - 1)
                    po, cols = bank[6 + j % 2][:, :], slice(j * P, (j + 1) * P)
                    product(po, lambda n, c: fhm[n][:, 0, c, cols], lambda n, c: F2[n][:, 0, c, :],
                            stop=False)
                    for n in range(2):
                        last = pe.matmul(po, maskT[:, b1_, cols], fb2s[:, n, :], start=False, stop=n == 1)
                    last.then_inc(f_h2, 1)

                if active(g, 1, NG):
                    pe.wait_ge(f_tl, 4 * g)
                    for c in range(KC):
                        need(pe, f_re, 4 * (g - 1) + c - 1)
                        product(bank[2 + c % 2][:, :], lambda n, i: F1[n][:, 0, i, c * P:(c + 1) * P],
                                lambda n, i: fxT[n][:, b1_, i, :]).then_inc(f_h1, 1)
                        if c == 0:
                            pe.wait_ge(f_mtc, g)
                        need(pe, f_hm, 4 * (g - 1) + c)
                        pe.matmul(bank[4][:, :], expand[:, c, :], maskT[:, b1_, :], start=True, stop=True
                                  ).then_inc(f_m, 1)
                if active(g, 0, NG):
                    for j in range(TG):
                        pe.wait_ge(f_xn, 4 * g + j + 1)
                        if j == 3:
                            need(pe, f_hm, 4 * g)
                        turn_tile(bank[turned[j]], fa[:, b, j, :]).then_inc(f_tr, 1)
                if active(g, 1, NG):
                    pe.wait_ge(f_hl, 4 * g)
                second_layer(0)
                if active(g, 0, NG):
                    pe.wait_ge(f_tl, 4 * (g + 1))
                    product(bank[5][0:EXP, :], lambda n, c: wrs[:, n, c, :],
                            lambda n, c: fxT[n][:, b, c, :]).then_inc(f_r, 1)
                second_layer(1)
                if active(g, 0, NG):
                    need_apart(pe, f_l, g + 1)
                    for j in range(TG):
                        last = pe.transpose(bank[4][:, j * EXP:(j + 1) * EXP], lgT[:, j * P:(j + 1) * P],
                                            ident[0:EXP, 0:EXP])
                    last.then_inc(f_lt, 1)
                second_layer(2)
                second_layer(3)
                if active(g, 0, NG):
                    pe.wait_ge(f_oh, g + 1)
                    for j in range(TG):
                        last = pe.transpose(bank[5][0:EXP, j * P:(j + 1) * P], onehot[:, j, :], ident[:, :])
                    last.then_inc(f_mt, 1)
            quad_turns(pe, ffn, 1)


def kernel(x, src, dst, L0_gnn_label, L0_gnn_W1_l, L0_gnn_W1_r, L0_gnn_b1, L0_gnn_W2_l, L0_gnn_W2_r,
           L0_gnn_b2, L0_mix_w_qkv, L0_mix_proj_mat, L0_mix_w_proj, L0_mix_b_proj, L0_ffn_Wr, L0_ffn_br,
           L0_ffn_W1, L0_ffn_b1, L0_ffn_W2, L0_ffn_b2):
    import numpy as np
    import concourse.bacc as bacc
    from concourse.bass_utils import run_bass_kernel_spmd

    def lay(a):
        return np.ascontiguousarray(a)

    p = np.arange(P)
    xp = np.zeros((NP, D), np.float32)
    xp[:N] = x
    srcp = np.zeros(NP, np.int32)
    srcp[:N] = src
    dstp = (TRASH + np.arange(NP) // TG % P).astype(np.int32)
    dstp[:N] = dst
    qkv = np.asarray(L0_mix_w_qkv)
    assert NP - N <= GROUP and N % TG == 0
    arrays = {
        "x": xp, "src": srcp, "dst": dstp,
        "w1lT": lay(np.asarray(L0_gnn_W1_l).T), "w1rT": lay(np.asarray(L0_gnn_W1_r).T),
        "b1": lay(np.asarray(L0_gnn_b1).reshape(KC, P).T),
        "w2lT": lay(np.asarray(L0_gnn_W2_l).T), "w2rT": lay(np.asarray(L0_gnn_W2_r).T),
        "b2": lay(L0_gnn_b2).reshape(1, D),
        "wqT": lay(qkv[:, 0:D].T), "wkT": lay(qkv[:, D:2 * D].T), "wv": lay(qkv[:, 2 * D:3 * D]),
        "pmat": lay(L0_mix_proj_mat), "wproj": lay(L0_mix_w_proj),
        "bproj": lay(L0_mix_b_proj).reshape(1, D),
        "wr": lay(L0_ffn_Wr), "br": lay(L0_ffn_br).reshape(EXP, 1),
        "f1": lay(np.asarray(L0_ffn_W1).transpose(1, 0, 2)).reshape(D, EXP * EH),
        "fb1": lay(np.asarray(L0_ffn_b1).reshape(KC, P).T),
        "f2": lay(L0_ffn_W2).reshape(EXP * EH, D), "fb2": lay(L0_ffn_b2),
        "ident_in": np.eye(P, dtype=np.float32),
        "tri_in": (p[None, :] < p[:, None]).astype(np.float32),
        "bmask_in": (p[None, :] // HD == p[:, None] // HD).astype(np.float32),
        "valid_in": np.repeat(np.stack([p >= 0, NP - GROUP + TG * p < N], axis=1), 2,
                              axis=1).astype(np.float32),
        "trash_in": (TRASH + p[:, None]).astype(np.float32),
        "expand_in": (np.arange(EXP * EH).reshape(1, KC, P) // EH
                      == np.arange(EXP)[:, None, None]).astype(np.float32),
        "iota_in": np.tile(np.arange(EXP, dtype=np.float32), (P, 1)),
    }
    nc = bacc.Bacc("TRN2", target_bir_lowering=False, num_devices=1)
    feeds, args = {}, {}
    for name, a in arrays.items():
        feeds["in_" + name] = a
        args[name] = nc.dram_tensor("in_" + name, a.shape, mybir.dt.from_np(a.dtype),
                                    kind="ExternalInput").ap()
    out = nc.dram_tensor("out", (NP, D), F32, kind="ExternalOutput").ap()
    build(nc, out=out, **args)
    got = run_bass_kernel_spmd(nc, [feeds], core_ids=[0])
    return got.results[0]["out"][:N]
```

```python
from contextlib import ExitStack

import concourse.bass as bass
from concourse import mybir

P = 128
D = 512
KC = D // P
TG = 4
GROUP = TG * P
N = 10000
NG = 4 * -(-N // (4 * GROUP))
NP = NG * GROUP
NT = NG * TG
PAIRS = NG // 2
TRASH = NP - P
HEADS, HD = 8, 64
EXP, EH = 8, 64
SLOTS = 21
AW = 520
LOW = 32
STACK = LOW + EXP
EPS = 1e-5

ALU = mybir.AluOpType
ACT = mybir.ActivationFunctionType
F32 = mybir.dt.float32
F32R = mybir.dt.float32r
I32 = mybir.dt.int32
U32 = mybir.dt.uint32


def need(eng, sem, value):
    if not (isinstance(value, int) and value <= 0):
        eng.wait_ge(sem, value)


def active(t, lag, count):
    return not isinstance(t, int) or 0 <= t - lag < count


def turns(eng, body, tail, head=1, last=0):
    for k in range(8 * head):
        body(k // 8, k % 8)
    with eng.Fori(head, PAIRS - last) as it:
        for k in range(8):
            body(it, k)
    for k in range(8 * last):
        body(PAIRS - last + k // 8, k % 8)
    for k in range(tail):
        body(PAIRS, k)


def group_turns(eng, body, tail, head=1):
    for b in range(2 * head):
        body(b // 2, b % 2)
    with eng.Fori(head, PAIRS) as it:
        for b in range(2):
            body(it, b)
    for b in range(tail):
        body(PAIRS + b // 2, b % 2)


def quad_turns(eng, body, tail, last=0):
    for k in range(4):
        body(0, k)
    with eng.Fori(1, NG // 4 - last) as it:
        for k in range(4):
            body(it, k)
    for k in range(4 * last):
        body(NG // 4 - last + k // 4, k % 4)
    for k in range(tail):
        body(NG // 4, k)


def lagged(turn, k, lag, per=8):
    return turn + (k - lag) // per, (k - lag) % per


def build(nc, x, src, dst, w1lT, w1rT, b1, w2lT, w2rT, b2, wqT, wkT, wv, pmat, wproj, bproj,
          wr, br, f1, fb1, f2, fb2, ident_in, tri_in, bmask_in, valid_in, trash_in, expand_in,
          iota_in, out):
    with ExitStack() as ctx:
        def sb(name, shape, dt=F32):
            return ctx.enter_context(nc.sbuf_tensor(name, shape, dt))

        def sem(name):
            return ctx.enter_context(nc.semaphore(name))

        xnT_d = [nc.dram_tensor(f"xnT_{n}_d", [NG, P, KC * GROUP], F32) for n in ("high", "low")]
        hT_d = [nc.dram_tensor(f"hT_{n}_d", [NG, P, KC * GROUP], F32) for n in ("high", "low")]
        wq_d, w2r_d, m_d, f1_d, f2_d = (
            [nc.dram_tensor(f"{w}_{n}_d", [P, KC * D], F32) for n in ("high", "low")]
            for w in ("wq", "w2r", "m", "f1", "f2"))
        agg1_d = nc.dram_tensor("agg1_d", [NP, AW], F32)
        agg2_d = nc.dram_tensor("agg2_d", [NP, D], F32)
        y_d = nc.dram_tensor("y_d", [NP, D], F32)
        part_d = nc.dram_tensor("part_d", [NG, P, TG * D], F32)
        agg1_g = agg1_d.ap().rearrange("(g p j) w -> g p (j w)", p=P, j=TG)
        agg2_g = agg2_d.ap().rearrange("(g p j) w -> g p (j w)", p=P, j=TG)
        y_g = y_d.ap().rearrange("(g p j) w -> g p (j w)", p=P, j=TG)
        x_g = x.rearrange("(g p j) w -> g p (j w)", p=P, j=TG)
        out_g = out.rearrange("(g p j) w -> g p (j w)", p=P, j=TG)
        src_g = src.rearrange("(g p j) -> g p j", p=P, j=TG)
        dst_g = dst.rearrange("(g p j) -> g p j", p=P, j=TG)
        dst_row = dst.rearrange("(g a e) -> g a e", a=1, e=GROUP)

        bank = [ctx.enter_context(nc.psum_tensor(f"bank{i}", [P, D], F32)) for i in range(8)]

        ident = sb("ident", [P, P])
        tri = sb("tri", [P, P])
        bmask = sb("bmask", [P, P])
        valid = sb("valid", [P, 4], F32R)
        trash = sb("trash", [P, 1])
        iota = sb("iota", [P, STACK])
        b1c = sb("b1c", [P, KC])
        fb1c = sb("fb1c", [P, KC])
        brc = sb("brc", [2 * EXP, 1])
        bias = sb("bias", [P, D])
        KS = sb("KS", [P, KC, P])
        ksum = sb("ksum", [P, KC])
        rdeg = sb("rdeg", [P, NT])

        arena = sb("arena", [P, SLOTS, TG * D])
        base = nc.sbuf_base - SLOTS * TG * D * 4

        def at(name, first, count, dt=F32, shape=None):
            return nc.alloc_sbuf_tensor_at(name, shape or [P, count, TG, D], dt,
                                           offset=base + int(first * TG * D * 4))

        def halves(name, first, count=1):
            return [at(f"{name}_high", first, count, F32R), at(f"{name}_low", first + count, count, F32R)]

        wkTs, wqTs = at("wkTs", 13, 1), at("wqTs", 14, 1)
        blockP = at("blockP", 15, 1, shape=[P, KC, P])
        wqs = halves("wq_made", 17)
        ax, axn = at("a_x", 0, 2), at("a_xn", 6, 1)
        xT = halves("xnT", 2, 2)
        axr, aph = halves("a_xn_rows", 7), halves("a_phi", 9)
        Wk = halves("Wk", 11)
        W1r, W1l, W2l = halves("W1r", 13), halves("W1l", 15), halves("W2l", 17)
        raw = at("raw_weight", 19, 1)
        spare = [at("spare_high", 20, 1, F32R), at("spare_low", 19, 1, F32R)]
        wvs, wps = at("wvs", 19, 1), at("wps", 20, 1)
        krow = at("key_sums", 1.5, 1, shape=[2, D])
        K2T, kvT = at("K2T", 0, 1), at("kvT", 1, 1, shape=[P, KC, P])
        Mf = halves("M_made", 19)
        by, baT, bhT = at("b_y", 0, 2), halves("aggT", 6), halves("hT_made", 8)
        bagg = at("b_agg", 10, 3, shape=[P, 2, TG, AW])
        Wq = halves("Wq", 19)
        mx_, mhT, mqz = at("m_x", 0, 2), halves("hT", 6, 2), halves("qz", 10, 2)
        M, W2r = halves("M", 15), halves("W2r", 17)
        fx, fa = at("f_x2", 2, 4), at("f_xn", 19, 2)
        F1, F2 = halves("F1", 6), halves("F2", 8)
        fxT, frelu, fhm = halves("x2T", 10, 2), at("f_relu", 15, 1), halves("masked", 16)
        maskT = at("maskT", 18, 1, F32R, [STACK, 2, GROUP])
        lgT = at("logitsT", 0, 1, shape=[2 * EXP, GROUP])
        craw = at("ffn_raw", 5, 1, shape=[P, 4, D])
        fb2s = at("fb2_halves", 14, 1, F32R, [STACK, D])
        expand = at("expand", 14.25, 1, F32R, [EXP, KC, P])
        wrs = at("wr_halves", 14.5, 1, F32R, [P, KC, 2, EXP])

        def router(name, place, cols, dt=F32):
            return nc.alloc_sbuf_tensor_at(name, [P, TG, cols], dt,
                                           offset=base + (14 * TG * D + 2 * D + 128 + place * TG * EXP) * 4)

        lg, mx, ix, lg2 = (router("logit", 0, EXP), router("mx", 1, 8), router("ix", 2, 8, U32),
                           router("logit_halves", 8, 2 * EXP))
        ixf, topd, tope, gate, rtop = (router(n, 3 + i, 1) for i, n in
                                       enumerate(("ixf", "topd", "tope", "gate", "rtop")))
        onehot = router("onehot", 10, STACK)

        esrc = sb("esrc", [P, 2, TG], I32)
        edst = sb("edst", [P, 2, TG], I32)
        erow = sb("erow", [P, 2, GROUP], I32)
        dstf = sb("dstf", [P, 2, TG])
        todump = sb("todump", [P, 2, TG])
        G = sb("G", [P, 4, D])
        G_low = nc.alloc_sbuf_tensor_at("G_low", [P, 4, D], F32R, offset=nc.sbuf_base - 4 * D * 4)
        S = sb("S", [P, 4, P], F32R)
        Sj = sb("Sj", [P, P])
        cnt = sb("cnt", [P, 4])
        cnt1 = sb("cnt1", [P, 4])
        eidx = sb("eidx", [P, 4, 1], I32)
        O = sb("O", [P, 4, AW])
        est = sb("est", [P, 6])

        st = sb("st", [P, 6])
        mv = sb("mv", [P, TG, 2])
        veps = sb("veps", [P, TG])
        rs = sb("rs", [P, TG])
        nhalf = sb("nhalf", [P, TG])
        low = sb("low", [P, 4, D])
        G_high = (nc.alloc_sbuf_tensor_at("G_high_keys", [P, 2, D], F32R, offset=nc.sbuf_base - 2 * D * 4),
                  at("G_high_mix", 14, 1, F32R, [P, 4, D]))
        rd = sb("rd", [P, 2, TG])
        pd = sb("pd", [P, D])


        s_w = sem("weights_in")
        s_zero, s_valid, s_hi = sem("zero_ready"), sem("valid_in"), sem("weight_high")
        s_f = sem("expert_weights_in")
        s_raw, s_split, s_kept = sem("raw_weight_in"), sem("weight_split"), sem("split_weight_stored")
        s_wk, s_late, s_fw = sem("qk_weights_in"), sem("late_constants_in"), sem("fold_weights_in")
        s_wqst, s_mst, s_wq = sem("wq_stored"), sem("m_stored"), sem("wq_in")
        s_w2r, s_m, s_craw, s_csp = sem("w2r_in"), sem("m_in"), sem("ffn_raw_in"), sem("ffn_raw_split")
        s_z = sem("zeroed")
        s_prep = sem("prepared")

        def prepared(eng):
            eng.drain().then_inc(s_prep, 1)
            eng.wait_ge(s_prep, 5)

        zero = sb("zero", [P, AW // 4])

        def clear(eng, agg_g, g, width, cleared):
            eng.dma_start(agg_g[g].rearrange("p (q w) -> p q w", w=width // 4),
                          zero[:, None, 0:width // 4].to_broadcast([P, 4 * TG, width // 4])
                          ).then_inc(cleared, 16)

        s_past = {}

        def need_apart(eng, sem, value):
            need(eng, sem, value)
            if not isinstance(value, int):
                eng.sem_inc(s_past[eng.engine], 1)

        e_in = [sem(f"edge_lists_in{b}") for b in range(2)]
        e_f = sem("edge_targets_float")
        e_td = sem("edge_trash_offset")
        e_g = [sem(f"edge_gathered{i}") for i in range(4)]
        e_cnt, e_cnt1 = sem("edge_repeats"), sem("edge_repeated")
        e_st = sem("edge_stats")
        e_s, e_n = sem("edge_tile_ready"), sem("edge_sources_normalised")
        e_gh, e_gl = sem("edge_sources_high"), sem("edge_sources_low")
        e_mm = sem("edge_summed")
        e_o = sem("edge_sums_out")
        e_sc = sem("edge_scattered")
        s_z1, s_z2 = sem("agg1_cleared"), sem("agg2_cleared")

        def flat(buf, b):
            return buf[:, b].rearrange("p c n -> p (c n)").bitcast(F32)

        def low_half(eng, out_, full, high):
            return eng.tensor_tensor(out_, full, high.bitcast(F32), ALU.subtract)

        def pair(name):
            return [sem(f"{name}{b}") for b in range(2)]

        a_x, a_st = pair("keys_x_in"), pair("keys_xnT_stored")
        a_s1, a_s2, a_s3 = sem("keys_stats"), sem("keys_mean_var"), sem("keys_rstd")
        a_ve, f_ve = sem("keys_var_eps"), sem("ffn_var_eps")
        a_xn, a_tr, a_ev = sem("keys_xn"), sem("keys_transposed"), sem("keys_xnT")
        a_kp, a_min, a_exp = sem("keys_k"), sem("keys_min"), sem("keys_exp")
        a_phi, a_T = sem("keys_phi"), sem("keys_summed")
        a_xh, a_xl = sem("keys_xn_high"), sem("keys_xn_low")
        a_tl, a_ph, a_pl = sem("keys_xnT_low"), sem("keys_phi_high"), sem("keys_phi_low")
        k_pe = sem("weights_folded")
        k_hi, k_lo = sem("folded_high"), sem("folded_low")
        c_mh, c_ml = sem("fold_m_high"), sem("fold_m_low")
        b_al, b_hh, b_hl = sem("hid_aggT_low"), sem("hid_h_high"), sem("hid_h_low")
        m_qh, m_ql = sem("mix_qz_high"), sem("mix_qz_low")
        f_tl, f_hh, f_hl = sem("ffn_xnT_low"), sem("ffn_masked_high"), sem("ffn_masked_low")
        c_kr = sem("fold_key_sums_turned")
        c_k2, c_kv, c_kvc, c_m = sem("fold_k2"), sem("fold_kv"), sem("fold_kv_kept"), sem("fold_m")
        b_xt, b_agg, b_yst = (pair(n) for n in ("hid_xnT_in", "hid_agg_in", "hid_y_stored"))
        b_hst = sem("hid_h_stored")
        b_d, b_r, b_ag = sem("hid_degree"), sem("hid_rdegree"), sem("hid_mean")
        b_tr, b_ev, b_h, b_th = sem("hid_transposed"), sem("hid_aggT"), sem("hid_h"), sem("hid_tanh")
        b_y, b_yo = sem("hid_y"), sem("hid_y_out")
        m_xt, m_ht, m_x, m_st = (pair(n) for n in ("mix_xnT_in", "mix_hT_in", "mix_x_in",
                                                   "mix_stored"))
        m_q, m_min, m_exp, m_phi = sem("mix_q"), sem("mix_min"), sem("mix_exp"), sem("mix_phi")
        m_den, m_z, m_qz, m_xb = sem("mix_den"), sem("mix_z"), sem("mix_qz"), sem("mix_x_bias")
        m_p, m_po = sem("mix_product"), sem("mix_part")
        f_p, f_st = ([sem(f"{n}{k}") for k in range(4)] for n in ("ffn_part_in", "ffn_stored"))
        f_a, f_lt = pair("ffn_agg_in"), sem("ffn_logits_turned")
        f_rd, f_x2 = sem("ffn_rdegree"), sem("ffn_x2")
        f_s1, f_s2, f_s3 = sem("ffn_stats"), sem("ffn_mean_var"), sem("ffn_rstd")
        f_xn, f_tr, f_ev, f_r = sem("ffn_xn"), sem("ffn_transposed"), sem("ffn_xnT"), sem("ffn_logits")
        f_l, f_mx, f_ix, f_ixf = sem("ffn_logits_b"), sem("ffn_max"), sem("ffn_index"), sem("ffn_indexf")
        f_d, f_e, f_g, f_oh = sem("ffn_top"), sem("ffn_top_exp"), sem("ffn_gate"), sem("ffn_onehot")
        f_rt, f_lg = sem("ffn_top_reciprocal"), sem("ffn_logits_kept")
        f_mt, f_mtc, f_h1, f_re = sem("ffn_maskT"), sem("ffn_maskT_kept"), sem("ffn_h"), sem("ffn_relu")
        f_m, f_hm, f_h2, f_out = sem("ffn_mask"), sem("ffn_masked"), sem("ffn_product"), sem("ffn_out")

        for e in (nc.vector, nc.gpsimd, nc.tensor):
            s_past[e.engine] = sem(f"wait_passed_{len(s_past)}")

        block = ctx.enter_context(nc.Block())

        def edge_load(sp, ph, turn, b):
            g = 2 * turn + b
            need(sp, e_s, ph * NT + 4 * g - 4)
            need(sp, e_gl, ph * NT + 4 * g - 4)
            for to, of in ((esrc[:, b, :], src_g[g]), (edst[:, b, :], dst_g[g]),
                           (erow[:, b, :], dst_row[g].to_broadcast([P, GROUP]))):
                sp.dma_start(to, of).then_inc(e_in[b], 16)

        def edge_gather(pool, ph, turn, k, table):
            t = 8 * turn + k
            if active(t, 0, NT):
                b, j = k // 4, k % 4
                if j == 0:
                    need_apart(pool, e_in[b], 48 * (ph * PAIRS + turn + 1))
                need_apart(pool, e_mm, ph * NT + t - 3)
                pool.indirect_dma_start(G[:, j, :], None, table,
                                        bass.IndirectOffsetOnAxis(ap=esrc[:, b, j:j + 1], axis=0)
                                        ).then_inc(e_g[j], 16)

        def edge_scatter(pool, ph, turn, k, agg, width):
            t = 8 * turn + k
            if active(t, 4, NT):
                j = (k - 4) % 4
                need_apart(pool, e_o, ph * NT + t - 3)
                need_apart(pool, e_sc, 16 * (ph * NT + t - 4))
                pool.indirect_dma_start(agg, bass.IndirectOffsetOnAxis(ap=eidx[:, j, 0:1], axis=0),
                                        O[:, j, 0:width], None, compute_op=ALU.add).then_inc(e_sc, 16)

        def edge_dve(dve, ph, turn, k):
            t = 8 * turn + k
            if not active(t, 2, NT):
                return
            turn1, kk = lagged(turn, k, 2)
            b, j = kk // 4, kk % 4
            u, ug = ph * NT + t - 1, ph * NG + 2 * turn1 + b
            if j == 0:
                dve.wait_ge(e_in[b], 48 * (ph * PAIRS + turn1 + 1))
                dve.tensor_copy(dstf[:, b, :], edst[:, b, :]).then_inc(e_f, 1)
                dve.wait_ge(e_f, ug + 1)
                dve.tensor_scalar(todump[:, b, :], dstf[:, b, :], -1.0, trash[:, 0:1], ALU.mult, ALU.add
                                  ).then_inc(e_td, 1)
            need(dve, e_mm, u - 4)
            need(dve, e_sc, 16 * (u - 4))
            row = erow[:, b, j:GROUP:TG]
            dve.scalar_tensor_tensor(Sj[:, :], row, dstf[:, b, j:j + 1], tri[:, :], ALU.is_equal,
                                     ALU.mult, accum_out=cnt[:, j:j + 1]).then_inc(e_cnt, 1)
            dve.tensor_scalar(S[:, j, :], row, dstf[:, b, j:j + 1], 0.0, ALU.is_equal, ALU.add,
                              accum_out=O[:, j, D:D + 1])
            dve.wait_ge(e_cnt, u)
            dve.tensor_scalar(cnt1[:, j:j + 1], cnt[:, j:j + 1], 1.0, None, ALU.min).then_inc(e_cnt1, 1)
            dve.wait_ge(e_cnt1, u)
            if j == 0:
                dve.wait_ge(e_td, ug + 1)
            dve.scalar_tensor_tensor(eidx[:, j, :], cnt1[:, j:j + 1], todump[:, b, j:j + 1],
                                     dstf[:, b, j:j + 1], ALU.mult, ALU.add).then_inc(e_s, 1)

        def edge_pe(pe, ph, turn, k, psum):
            t = 8 * turn + k
            if active(t, 3, NT):
                j = (k - 3) % 4
                pe.wait_ge(e_s, ph * NT + t - 2)
                need(pe, e_o, ph * NT + t - 3)
                pe.wait_ge(e_gl, ph * NT + t - 2)
                high = G_high[ph][:, j % (2 + 2 * ph), :]
                pe.matmul(psum, S[:, j, :], high, start=True, stop=False)
                pe.matmul(psum, S[:, j, :], G_low[:, j, :], start=False, stop=True).then_inc(e_mm, 1)

        def edge_act(act, ph, turn, k, psum):
            t = 8 * turn + k
            if active(t, 2, NT):
                turn2, kk = lagged(turn, k, 2)
                j = kk % 4
                if ph == 0:
                    act.wait_ge(e_n, t - 1)
                else:
                    act.wait_ge(e_g[j], 16 * (NT // 4 + 2 * turn2 + kk // 4 + 1))
                need(act, e_mm, ph * NT + t - 3)
                act.copy(G_high[ph][:, j % (2 + 2 * ph), :], G[:, j, :]).then_inc(e_gh, 1)
            if active(t, 3, NT):
                j = (k - 3) % 4
                act.wait_ge(e_mm, ph * NT + t - 2)
                need(act, e_sc, 16 * (ph * NT + t - 6))
                act.copy(O[:, j, 0:D], psum).then_inc(e_o, 1)

        def edge_low(pool, ph, turn, k):
            t = 8 * turn + k
            if active(t, 2, NT):
                j = (k - 2) % 4
                pool.wait_ge(e_gh, ph * NT + t - 1)
                low_half(pool, G_low[:, j, :], G[:, j, :], G_high[ph][:, j % (2 + 2 * ph), :]
                         ).then_inc(e_gl, 1)

        s_bp, s_bias = sem("feature_blocks_in"), sem("biases_added")
        s_zf = s_bias

        def kpn(w):
            return w.rearrange("(c p) n -> p c n", p=P)

        first = [(wkTs[:, 0], kpn(wkT)), (wqTs[:, 0], kpn(wqT))]
        consts = [(ident[:], ident_in), (tri[:], tri_in), (trash[:], trash_in)]
        late = [(bmask[:], bmask_in), (iota[:], iota_in), (b1c[:], b1), (fb1c[:], fb1),
                (brc[:], br), (bias[:], b2.to_broadcast([P, D])),
                (pd[:], bproj.to_broadcast([P, D]))]
        splits = [(w1rT, W1r, None), (w1lT, W1l, None), (w2lT, W2l, None),
                  (w2rT, None, w2r_d), (f1, None, f1_d), (f2, None, f2_d)]

        turned = (0, 1, 5, 2)
        means = (0, 1, 6, 7)

        split_at = (1, 6, 11, 16, 22, 28)
        raw_at = {2: 1, 3: 2, 4: 3, 5: 4, 7: 5, 8: 6}
        quarter = {at_ + q: (i, q) for i, at_ in enumerate(split_at) for q in range(4)}

        @block.sync
        def _(sp):
            for to, of in first:
                sp.dma_start(to, of).then_inc(s_wk, 16)
            sp.wait_ge(s_z, 1)
            for h in range(HEADS):
                o = HD * (h % 2)
                sp.dma_start(blockP[o:o + HD, h // 2, o:o + HD], pmat[h]).then_inc(s_bp, 16)
            sp.dma_start(low[:, 0, 0:4], valid_in).then_inc(s_valid, 16)
            for b in range(2):
                edge_load(sp, 0, 0, b)
                sp.dma_start(flat(ax, b), x_g[b]).then_inc(a_x[b], 16)
            for to, of in consts:
                sp.dma_start(to, of).then_inc(s_w, 16)
            sp.dma_start(raw[:, 0], kpn(splits[0][0])).then_inc(s_raw, 16)
            sp.drain().then_inc(s_prep, 1)
            sp.wait_ge(s_zero, 1)
            sp.wait_ge(e_g[3], 16)
            for g in range(NG):
                clear(sp, agg1_g, g, AW, s_z1)
            sp.wait_ge(k_lo, 2 * KC)
            for n in range(2):
                sp.dma_start(wq_d[n][:], flat(wqs[n], 0)).then_inc(s_wqst, 16)
            for to, of in late:
                sp.dma_start(to, of).then_inc(s_late, 16)
            sp.wait_ge(s_prep, 5)

            def keys(turn, b):
                g = 2 * turn + b
                if isinstance(g, int) and g < 2:
                    return
                sp.wait_ge(a_xn, 4 * (g - 1))
                sp.dma_start(flat(ax, b), x_g[g]).then_inc(a_x[b], 16)
                edge_load(sp, 0, turn, b)
                if isinstance(g, int) and g in raw_at:
                    i = raw_at[g]
                    sp.wait_ge(s_split, 4 * i)
                    if splits[i - 1][2] is not None:
                        for n in range(2):
                            sp.dma_start(splits[i - 1][2][n][:], flat(spare[n], 0)).then_inc(s_kept, 16)
                        sp.wait_ge(s_kept, 32 * (i - 3))
                    if i < len(splits):
                        sp.dma_start(raw[:, 0], kpn(splits[i][0])).then_inc(s_raw, 16)
                    else:
                        sp.dma_start(wvs[:, 0], kpn(wv)).then_inc(s_fw, 16)
                        sp.dma_start(wps[:, 0], kpn(wproj)).then_inc(s_fw, 16)
            group_turns(sp, keys, 0, head=5)
            for b in range(2):
                sp.wait_ge(a_st[b], 32 * PAIRS)
            sp.wait_ge(a_T, NT)
            sp.wait_ge(e_sc, 16 * NT)

            def mix_xnT(g, turn, b):
                for n in range(2):
                    sp.dma_start(flat(xT[n], b), xnT_d[n][g]).then_inc(m_xt[b], 16)
                edge_load(sp, 1, turn, b)

            def hidden(turn, b):
                g = 2 * turn + b
                if isinstance(g, int) and g == NG:
                    sp.wait_ge(b_h, 4 * NG)
                    mix_xnT(0, 0, 0)
                if active(g, 0, NG):
                    need(sp, b_tr, 4 * (g - 1))
                    sp.dma_start(bagg[:, b].rearrange("p j w -> p (j w)"), agg1_g[g]).then_inc(b_agg[b], 16)
                    need(sp, b_h, 4 * (g - 1))
                    for n in range(2):
                        sp.dma_start(flat(xT[n], b), xnT_d[n][g]).then_inc(b_xt[b], 16)
                if isinstance(g, int) and g == 1:
                    sp.wait_ge(c_ml, KC)
                    for n in range(2):
                        sp.dma_start(m_d[n][:], flat(Mf[n], 0)).then_inc(s_mst, 16)
                    sp.wait_ge(s_mst, 32)
                    for n in range(2):
                        sp.dma_start(flat(Wq[n], 0), wq_d[n][:]).then_inc(s_wq, 16)
                if active(g, 1, NG):
                    sp.wait_ge(b_hl, 4 * g)
                    for n in range(2):
                        sp.dma_start(hT_d[n][g - 1], flat(bhT[n], 0)).then_inc(b_hst, 16)
                    sp.wait_ge(b_yo, 4 * g)
                    sp.dma_start(y_g[g - 1], flat(by, 1 - b)).then_inc(b_yst[1 - b], 16)
            group_turns(sp, hidden, 1)
            for b in range(2):
                sp.wait_ge(b_yst[b], 16 * PAIRS)
            sp.wait_ge(b_hst, 32 * NG)
            mix_xnT(1, 0, 1)

            def paced(n):
                need(sp, e_mm, NT + n - 2)

            def mix(turn, b):
                g = 2 * turn + b
                if active(g, 0, NG) and not (isinstance(g, int) and g < 2):
                    if isinstance(g, int) and g == 2:
                        paced(7)
                    need(sp, m_q, 4 * (g - 1))
                    mix_xnT(g, turn, b)
                if isinstance(g, int) and g == 0:
                    for n in range(2):
                        paced(n)
                        sp.dma_start(flat(W2r[n], 0), w2r_d[n][:]).then_inc(s_w2r, 16)
                    for n in range(2):
                        paced(n + 2)
                        sp.dma_start(flat(M[n], 0), m_d[n][:]).then_inc(s_m, 16)
                if active(g, 3, NG):
                    sp.wait_ge(m_po, 4 * (g - 2))
                    sp.dma_start(part_d[g - 3], flat(mx_, 1 - b)).then_inc(m_st[1 - b], 16)
                if active(g, 1, NG):
                    turn1, b1_ = lagged(turn, b, 1, 2)
                    need(sp, m_p, 4 * (g - 2))
                    for n in range(2):
                        if isinstance(g, int) and g == 1:
                            paced(n + 4)
                        sp.dma_start(flat(mhT[n], b1_), hT_d[n][g - 1]).then_inc(m_ht[b1_], 16)
                    if isinstance(g, int) and g == 1:
                        paced(6)
                    need(sp, m_st[b1_], 16 * turn1)
                    sp.dma_start(flat(mx_, b1_), x_g[g - 1]).then_inc(m_x[b1_], 16)
                if isinstance(g, int) and g == NG:
                    sp.wait_ge(m_q, NT)
                    sp.wait_ge(e_sc, 16 * 2 * NT)
                    sp.dma_start(craw[:, 0, 0:KC * EXP].rearrange("p (c e) -> p c e", c=KC), kpn(wr)
                                 ).then_inc(s_craw, 16)
                    sp.dma_start(craw[0:EXP, 1, :], fb2).then_inc(s_craw, 16)
                    sp.dma_start(craw[LOW:STACK, 1, :], fb2).then_inc(s_craw, 16)
                    sp.dma_start(craw[0:EXP, 2, :], expand_in.rearrange("e c p -> e (c p)")).then_inc(s_craw, 16)
                    for i in range(2):
                        sp.dma_start(flat(fx, i), part_d[i]).then_inc(f_p[i], 16)
                        sp.dma_start(flat(fa, i), agg2_g[i]).then_inc(f_a[i], 16)
            group_turns(sp, mix, 3, head=2)
            for b in range(2):
                sp.wait_ge(m_st[b], 16 * PAIRS)
            sp.wait_ge(m_p, NT)
            for w, d in ((F1, f1_d), (F2, f2_d)):
                for n in range(2):
                    sp.dma_start(flat(w[n], 0), d[n][:]).then_inc(s_f, 16)
            sp.wait_ge(s_csp, 5)

            def ffn(turn, k):
                g, b = 4 * turn + k, k % 2
                if active(g, 0, NG) and not (isinstance(g, int) and g < 2):
                    need(sp, f_st[k], 16 * turn)
                    sp.dma_start(flat(fx, k), part_d[g]).then_inc(f_p[k], 16)
                    need(sp, f_tr, 4 * (g - 1))
                    sp.dma_start(flat(fa, b), agg2_g[g]).then_inc(f_a[b], 16)
                if active(g, 2, NG):
                    sp.wait_ge(f_out, 4 * (g - 1))
                    sp.dma_start(out_g[g - 2], flat(fx, (k - 2) % 4)).then_inc(f_st[(k - 2) % 4], 16)
            quad_turns(sp, ffn, 2)
            for k in range(4):
                sp.wait_ge(f_st[k], 16 * NG // 4)

        @block.gpsimd
        def _(pool):
            pool.memset(zero[:, :], 0.0).then_inc(s_zero, 1)
            pool.memset(nhalf[:, :], -0.5)
            pool.memset(O[:, :, :], 0.0)
            pool.memset(mv[:, :, :], 1.0)
            pool.wait_ge(s_valid, 16)
            pool.tensor_copy(valid[:, :], low[:, 0, 0:4])
            for j in range(TG):
                edge_gather(pool, 0, 0, j, x)
            prepared(pool)

            def split(i, q):
                high, lo = (h[:, 0, q, :] for h in splits[i][1] or spare)
                pool.wait_ge(s_hi, 4 * i + q + 1)
                low_half(pool, lo, raw[:, 0, q, :], high).then_inc(s_split, 1)

            def keys(turn, k):
                t = 8 * turn + k
                if active(t, 0, NT + 2):
                    need_apart(pool, a_s2, t + 1)
                    pool.tensor_scalar(veps[:, 0:2], mv[:, 0:2, 1], EPS, None, ALU.add).then_inc(a_ve, 1)
                    pool.wait_ge(a_ve, t + 1)
                    pool.tensor_tensor(rs[:, 0:2], veps[:, 0:2], nhalf[:, 0:2], ALU.pow).then_inc(a_s3, 1)
                if not (isinstance(t, int) and t < TG):
                    edge_gather(pool, 0, turn, k, x)
                if isinstance(t, int) and t == 4:
                    pool.wait_ge(s_z1, 16 * NG)
                edge_scatter(pool, 0, turn, k, agg1_d.ap(), AW)
                if active(t, 0, NT):
                    pool.wait_ge(a_xh, t + 1)
                    need(pool, a_T, t - 3)
                    low_half(pool, axr[1][:, 0, k % 4, :], axn[:, 0, k % 4, :], axr[0][:, 0, k % 4, :]
                             ).then_inc(a_xl, 1)
                edge_low(pool, 0, turn, k)
                if isinstance(t, int) and t in quarter:
                    split(*quarter[t])
            turns(pool, keys, 4, head=4)
            pool.wait_ge(s_late, 16 * len(late))
            pool.tensor_tensor(bias[:, :], bias[:, :], pd[:, :], ALU.add).then_inc(s_bias, 1)
            pool.wait_ge(e_sc, 16 * NT)
            pool.wait_ge(s_bias, 1)
            for b in range(2):
                pool.wait_ge(b_yst[b], 16 * PAIRS)
            pool.wait_ge(s_z2, 16 * NG)

            def step(turn, k):
                t = 8 * turn + k
                edge_gather(pool, 1, turn, k, y_d.ap())
                edge_scatter(pool, 1, turn, k, agg2_d.ap(), D)
                edge_low(pool, 1, turn, k)
                if active(t, 7, NT):
                    turn1, kk = lagged(turn, k, 7)
                    b, j = kk // 4, kk % 4
                    if j == 0:
                        pool.wait_ge(m_x[b], 16 * (turn1 + 1))
                    xr = mx_[:, b, j, :]
                    pool.tensor_tensor(xr, xr, bias[:, :], ALU.add).then_inc(m_xb, 1)
            turns(pool, step, 7)
            pool.wait_ge(e_sc, 16 * 2 * NT)

            pool.wait_ge(e_mm, 2 * NT)
            pool.tensor_scalar(fb2s[:, :], trash[0:STACK, 0:1].to_broadcast([STACK, D]), 0.0, None,
                               ALU.mult).then_inc(s_zf, 1)

            def ffn(turn, b):
                for j in range(TG):
                    t = 4 * (2 * turn + b) + j
                    need_apart(pool, f_s2, t + 1)
                    pool.tensor_scalar(veps[:, j:j + 1], mv[:, j, 1:2], EPS, None, ALU.add
                                       ).then_inc(f_ve, 1)
                    pool.wait_ge(f_ve, t + 1)
                    pool.tensor_tensor(rs[:, j:j + 1], veps[:, j:j + 1], nhalf[:, j:j + 1], ALU.pow
                                       ).then_inc(f_s3, 1)
            group_turns(pool, ffn, 0)

        @block.scalar
        def _(act):
            for i in range(2 * KC):
                act.wait_ge(k_pe, i + 1)
                act.copy((Wk if i < KC else wqs)[0][:, 0, i % KC, :], bank[i][:, :]).then_inc(k_hi, 1)
            prepared(act)

            def keys(turn, k):
                t, b, j = 8 * turn + k, k // 4, k % 4
                if active(t, 1, NT):
                    act.wait_ge(a_kp, t)
                    need(act, a_pl, t - 2)
                    lo = low[:, (k - 1) % 2, :]
                    act.activation(lo, bank[6][:, :], ACT.Relu, scale=-1.0).then_inc(a_min, 1)
                    act.wait_ge(a_min, t)
                    act.activation(lo, lo, ACT.Exp, scale=-1.0).then_inc(a_exp, 1)
                if active(t, 0, NT):
                    act.wait_ge(a_xn, t + 1)
                    need(act, a_T, t - 3)
                    act.copy(axr[0][:, 0, j, :], axn[:, 0, j, :]).then_inc(a_xh, 1)
                    act.wait_ge(a_tr, t + 1)
                    if j == 0:
                        need(act, a_kp, t - 4)
                        need(act, a_st[b], 32 * turn)
                    act.copy(xT[0][:, b, :, j * P:(j + 1) * P],
                             bank[5][:, :].rearrange("p (c n) -> p c n", c=KC)).then_inc(a_ev, 1)
                edge_act(act, 0, turn, k, bank[7][:, :])
                if active(t, 1, NT):
                    act.wait_ge(a_phi, t)
                    need(act, a_T, t - 4)
                    act.copy(aph[0][:, 0, (k - 1) % 4, :], low[:, (k - 1) % 2, :]).then_inc(a_ph, 1)
                if active(t, 0, NT) and j == 3:
                    act.wait_ge(a_tl, t + 1)
                    act.wait_ge(a_ev, t + 1)
                    for n in range(2):
                        act.dma_start(xnT_d[n][2 * turn + b], flat(xT[n], b)).then_inc(a_st[b], 16)
                    clear(act, agg2_g, 2 * turn + b, D, s_z2)
                if isinstance(t, int) and t in quarter:
                    i, q = quarter[t]
                    if q == 0:
                        act.wait_ge(s_raw, 16 * (i + 1))
                        if i == 2:
                            act.wait_ge(s_wqst, 32)
                    act.copy((splits[i][1] or spare)[0][:, 0, q, :], raw[:, 0, q, :]).then_inc(s_hi, 1)
            turns(act, keys, 3, head=4)
            act.wait_ge(a_T, NT)
            for i in range(KC // 2, KC):
                act.copy(K2T[:, 0, i, :], bank[i][:, :]).then_inc(c_k2, 1)
            for b in range(2):
                act.wait_ge(a_st[b], 32 * PAIRS)
            act.wait_ge(s_z2, 16 * NG)

            act.wait_ge(a_xl, NT)
            act.wait_ge(s_late, 16 * len(late))

            def hidden(turn, b):
                g = 2 * turn + b
                for j in range(TG):
                    act.wait_ge(b_tr, 4 * g + j + 1)
                    if j == 0:
                        need(act, b_h, 4 * g)
                    act.copy(baT[0][:, 0, :, j * P:(j + 1) * P],
                             bank[means[j]][:, :].rearrange("p (c n) -> p c n", c=KC)).then_inc(b_ev, 1)
                for o in range(KC):
                    act.wait_ge(b_h, 4 * g + o + 1)
                    need(act, b_hl, 4 * (g - 1) + o + 1)
                    act.activation(low[:, o, :], bank[2 + o % 2][:, :], ACT.Tanh,
                                   bias=b1c[:, o:o + 1]).then_inc(b_th, 1)
                    if o == 0:
                        need(act, b_y, 4 * g)
                        need(act, b_hst, 32 * g)
                    act.wait_ge(b_th, 4 * g + o + 1)
                    act.copy(bhT[0][:, 0, o, :], low[:, o, :]).then_inc(b_hh, 1)
            group_turns(act, hidden, 0)

            act.wait_ge(b_hl, 4 * NG)
            def mix(turn, k):
                t = 8 * turn + k
                if active(t, 1, NT):
                    act.wait_ge(m_q, t)
                    need(act, m_ql, t - 4)
                    lo = low[:, (k - 1) % 4, :]
                    act.activation(lo, bank[(k - 1) % 2][:, :], ACT.Relu, scale=-1.0).then_inc(m_min, 1)
                    act.wait_ge(m_min, t)
                    act.activation(lo, lo, ACT.Exp, scale=-1.0).then_inc(m_exp, 1)
                edge_act(act, 1, turn, k, bank[7][:, :])
                if active(t, 3, NT):
                    turn3, kk = lagged(turn, k, 3)
                    act.wait_ge(m_qz, t - 2)
                    need(act, m_p, 4 * (2 * turn3 + kk // 4 - 1))
                    act.copy(mqz[0][:, kk // 4, kk % 4, :], low[:, kk % 4, :]).then_inc(m_qh, 1)
            turns(act, mix, 3, head=2)

            act.wait_ge(m_st[0], 16 * PAIRS)
            act.wait_ge(s_zf, 2)
            act.wait_ge(s_craw, 64)
            raw_wr = craw[:, 0, 0:KC * EXP].rearrange("p (c e) -> p c e", c=KC)
            act.copy(wrs[:, :, 0, :], raw_wr).then_inc(s_csp, 1)
            act.copy(fb2s[LOW:STACK, :], craw[LOW:STACK, 1, :])
            act.copy(fb2s[0:EXP, :], craw[0:EXP, 1, :]).then_inc(s_csp, 1)
            act.copy(expand[:, :, :].rearrange("e c p -> e (c p)"), craw[0:EXP, 2, :]).then_inc(s_csp, 1)

            def ffn(turn, k):
                g, b = 4 * turn + k, k % 2
                if active(g, 1, NG):
                    for c in range(KC):
                        act.wait_ge(f_h1, 4 * (g - 1) + c + 1)
                        need(act, f_hl, 4 * (g - 2) + c + 1)
                        act.activation(frelu[:, 0, c, :], bank[2 + c % 2][:, :], ACT.Relu,
                                       bias=fb1c[:, c:c + 1]).then_inc(f_re, 1)
                        act.wait_ge(f_hm, 4 * (g - 1) + c + 1)
                        if c == 0:
                            need(act, f_h2, 4 * (g - 1))
                        act.copy(fhm[0][:, 0, c, :], frelu[:, 0, c, :]).then_inc(f_hh, 1)
                if active(g, 0, NG):
                    for j in range(TG):
                        act.wait_ge(f_tr, 4 * g + j + 1)
                        if j == 0:
                            need(act, f_h1, 4 * (g - 1))
                        act.copy(fxT[0][:, b, :, j * P:(j + 1) * P],
                                 bank[turned[j]][:, :].rearrange("p (c n) -> p c n", c=KC)
                                 ).then_inc(f_ev, 1)
                    act.wait_ge(f_r, g + 1)
                    need(act, f_lt, g)
                    act.activation(lgT[:, :], bank[5][0:2 * EXP, :], ACT.Identity, bias=brc[:, 0:1]
                                   ).then_inc(f_l, 1)
                    act.wait_ge(f_d, g + 1)
                    act.activation(tope[:, :, 0], topd[:, :, 0], ACT.Exp).then_inc(f_e, 1)
                    act.wait_ge(f_mt, g + 1)
                    act.copy(maskT[:, b, :], bank[5][0:STACK, :]).then_inc(f_mtc, 1)
            quad_turns(act, ffn, 1)

        @block.vector
        def _(dve):
            dve.memset(blockP[:, :, :], 0.0).then_inc(s_z, 1)
            for i in range(2 * KC):
                dve.wait_ge(k_hi, i + 1)
                w = Wk if i < KC else wqs
                low_half(dve, w[1][:, 0, i % KC, :], bank[i][:, :], w[0][:, 0, i % KC, :]).then_inc(k_lo, 1)
            prepared(dve)

            dve.wait_ge(s_w, 16 * len(consts))
            def keys(turn, k):
                t, b, j = 8 * turn + k, k // 4, k % 4
                if active(t, 0, NT):
                    if j == 0:
                        dve.wait_ge(a_x[b], 16 * (turn + 1))
                    xr = ax[:, b, j, :]
                    dve.bn_stats(st[:, :], xr).then_inc(a_s1, 1)
                if active(t, 2, NT):
                    turn2, kk = lagged(turn, k, 2)
                    dve.wait_ge(e_g[kk % 4], 16 * (2 * turn2 + kk // 4 + 1))
                    dve.bn_stats(est[:, :], G[:, kk % 4, :]).then_inc(e_st, 1)
                if active(t, 0, NT):
                    need_apart(dve, a_s1, t + 1)
                    last = dve.bn_aggr(mv[:, 0, :], st[:, :])
                if active(t, 2, NT):
                    need_apart(dve, e_st, t - 1)
                    last = dve.bn_aggr(mv[:, 1, :], est[:, :])
                if active(t, 0, NT + 2):
                    last.then_inc(a_s2, 1)
                edge_dve(dve, 0, turn, k)
                if active(t, 2, NT):
                    jj = (k - 2) % 4
                    dve.wait_ge(a_ph, t - 1)
                    need(dve, a_T, t - 5)
                    low_half(dve, aph[1][:, 0, jj, :], low[:, k % 2, :], aph[0][:, 0, jj, :]).then_inc(a_pl, 1)
                if active(t, 0, NT):
                    dve.wait_ge(a_s3, t + 1)
                    need(dve, a_tr, t - 3)
                    need(dve, a_xl, t - 3)
                    dve.tensor_scalar(axn[:, 0, j, :], xr, mv[:, 0, 0:1], rs[:, 0:1],
                                      ALU.subtract, ALU.mult).then_inc(a_xn, 1)
                if active(t, 2, NT):
                    dve.wait_ge(a_s3, t + 1)
                    Gj = G[:, (k - 2) % 4, :]
                    dve.tensor_scalar(Gj, Gj, mv[:, 1, 0:1], rs[:, 1:2], ALU.subtract, ALU.mult
                                      ).then_inc(e_n, 1)
                if active(t, 1, NT):
                    lo = low[:, (k - 1) % 2, :]
                    dve.wait_ge(a_exp, t)
                    dve.scalar_tensor_tensor(lo, bank[6][:, :], 0.0, lo, ALU.max, ALU.add).then_inc(a_phi, 1)
                if active(t, 0, NT):
                    dve.wait_ge(a_ev, t + 1)
                    low_half(dve, xT[1][:, b, :, j * P:(j + 1) * P],
                             bank[5][:, :].rearrange("p (c n) -> p c n", c=KC),
                             xT[0][:, b, :, j * P:(j + 1) * P]).then_inc(a_tl, 1)
            turns(dve, keys, 2)
            dve.wait_ge(a_T, NT)

            for i in range(KC // 2):
                dve.tensor_copy(K2T[:, 0, i, :], bank[i][:, :]).then_inc(c_k2, 1)
            dve.tensor_copy(krow[:, :], bank[4][0:2, :]).then_inc(c_k2, 1)
            dve.wait_ge(c_kr, 1)
            dve.tensor_copy(ksum[:, :], bank[5][:, 0:2 * KC:2]).then_inc(c_k2, 1)
            dve.wait_ge(c_k2, KC + 2)
            for c in range(KC):
                dve.tensor_scalar(KS[:, c, :], bmask[:, :], ksum[:, c:c + 1], None, ALU.mult)
            for c in range(KC):
                dve.wait_ge(c_kv, c + 1)
                dve.tensor_tensor(kvT[:, c, :], bank[4 + c][:, 0:P], bmask[:, :], ALU.mult
                                  ).then_inc(c_kvc, 1)
            for c in range(KC):
                dve.wait_ge(c_m, c + 1)
                dve.tensor_copy(Mf[0][:, 0, c, :], bank[c][:, :]).then_inc(c_mh, 1)
                dve.wait_ge(c_mh, c + 1)
                low_half(dve, Mf[1][:, 0, c, :], bank[c][:, :], Mf[0][:, 0, c, :]).then_inc(c_ml, 1)

            def hidden(turn, b):
                g = 2 * turn + b
                if active(g, 0, NG):
                    agg = bagg[:, b]
                    dve.wait_ge(b_agg[b], 16 * (turn + 1))
                    dve.tensor_scalar(rd[:, b, :], agg[:, :, D], 1.0, None, ALU.max).then_inc(b_d, 1)
                    dve.wait_ge(b_d, g + 1)
                    dve.reciprocal(rd[:, b, :], rd[:, b, :]).then_inc(b_r, 1)
                    dve.wait_ge(b_r, g + 1)
                    dve.tensor_copy(rdeg[:, bass.ds(4 * g, TG)], rd[:, b, :])
                    for j in range(TG):
                        dve.tensor_scalar(agg[:, j, 0:D], agg[:, j, 0:D], rd[:, b, j:j + 1], None,
                                          ALU.mult).then_inc(b_ag, 1)
                if active(g, 1, NG):
                    for o in range(KC):
                        dve.wait_ge(b_hh, 4 * (g - 1) + o + 1)
                        low_half(dve, bhT[1][:, 0, o, :], low[:, o, :], bhT[0][:, 0, o, :]).then_inc(b_hl, 1)
                if active(g, 0, NG):
                    for j in range(TG):
                        dve.wait_ge(b_ev, 4 * g + j + 1)
                        cols = slice(j * P, (j + 1) * P)
                        low_half(dve, baT[1][:, 0, :, cols],
                                 bank[means[j]][:, :].rearrange("p (c n) -> p c n", c=KC),
                                 baT[0][:, 0, :, cols]).then_inc(b_al, 1)
                if active(g, 1, NG):
                    turn1, b1_ = lagged(turn, b, 1, 2)
                    need(dve, b_yst[b1_], 16 * turn1)
                    for j in range(TG):
                        dve.wait_ge(b_y, 4 * (g - 1) + j + 1)
                        dve.tensor_copy(by[:, b1_, j, :], bank[4 + j % 2][:, :]).then_inc(b_yo, 1)
            group_turns(dve, hidden, 1, head=2)
            dve.wait_ge(s_bias, 1)

            def pre(turn, k, j):
                g, b = 4 * turn + k, k % 2
                if not active(g, 0, NG):
                    return
                x2, xn = fx[:, k, j, :], fa[:, b, j, :]
                t = 4 * g + j
                if j == 0:
                    dve.wait_ge(f_p[k], 16 * (turn + 1))
                    dve.wait_ge(f_a[b], 16 * (2 * turn + k // 2 + 1))
                    dve.tensor_copy(rd[:, b, :], rdeg[:, bass.ds(4 * g, TG)]).then_inc(f_rd, 1)
                    dve.wait_ge(f_rd, g + 1)
                dve.scalar_tensor_tensor(x2, xn, rd[:, b, j:j + 1], x2, ALU.mult, ALU.add
                                         ).then_inc(f_x2, 1)
                dve.wait_ge(f_x2, t + 1)
                dve.bn_stats(st[:, :], x2).then_inc(f_s1, 1)
                need_apart(dve, f_s1, t + 1)
                dve.bn_aggr(mv[:, j, :], st[:, :]).then_inc(f_s2, 1)

            def norm(turn, k, j):
                g = 4 * turn + k
                if active(g, 0, NG):
                    dve.wait_ge(f_s3, 4 * g + j + 1)
                    dve.tensor_scalar(fa[:, k % 2, j, :], fx[:, k, j, :], mv[:, j, 0:1],
                                      rs[:, j:j + 1], ALU.subtract, ALU.mult).then_inc(f_xn, 1)

            def mix(turn, k):
                t = 8 * turn + k
                if active(t, 4, NT):
                    kk = (k - 4) % 8
                    dve.wait_ge(m_qh, t - 3)
                    low_half(dve, mqz[1][:, kk // 4, kk % 4, :], low[:, kk % 4, :],
                             mqz[0][:, kk // 4, kk % 4, :]).then_inc(m_ql, 1)
                if active(t, 3, NT):
                    dve.wait_ge(m_den, t - 2)
                    need(dve, m_qz, t - 3)
                    dve.reciprocal(pd[:, :], bank[2][:, :]).then_inc(m_z, 1)
                    dve.wait_ge(m_z, t - 2)
                    lz = low[:, (k - 3) % 4, :]
                    dve.tensor_tensor(lz, lz, pd[:, :], ALU.mult).then_inc(m_qz, 1)
                if active(t, 1, NT):
                    lo, pq = low[:, (k - 1) % 4, :], bank[(k - 1) % 2][:, :]
                    dve.wait_ge(m_exp, t)
                    dve.scalar_tensor_tensor(lo, pq, 0.0, lo, ALU.max, ALU.add).then_inc(m_phi, 1)
                edge_dve(dve, 1, turn, k)
                if isinstance(t, int) and t == NT + 7:
                    for j in range(TG):
                        pre(0, 0, j)
                    for j in range(TG):
                        norm(0, 0, j)
                if active(t, 9, NT):
                    turn1, kk = lagged(turn, k, 9)
                    xr = mx_[:, kk // 4, kk % 4, :]
                    dve.wait_ge(m_p, t - 8)
                    dve.wait_ge(m_xb, t - 8)
                    dve.tensor_tensor(xr, bank[4 + kk % 2][:, :], xr, ALU.add).then_inc(m_po, 1)
            turns(dve, mix, 9, head=2)

            dve.wait_ge(s_csp, 3)
            low_half(dve, wrs[:, :, 1, :], craw[:, 0, 0:KC * EXP].rearrange("p (c e) -> p c e", c=KC),
                     wrs[:, :, 0, :]).then_inc(s_csp, 1)
            high = fb2s[LOW:STACK, :]
            low_half(dve, high, craw[LOW:STACK, 1, :], high).then_inc(s_csp, 1)

            def ffn(turn, k):
                g, b, k1 = 4 * turn + k, k % 2, (k - 1) % 4

                def out_tile(j):
                    dve.wait_ge(f_h2, 4 * (g - 1) + j + 1)
                    x2 = fx[:, k1, j, :]
                    dve.tensor_tensor(x2, bank[6 + j % 2][:, :], x2, ALU.add).then_inc(f_out, 1)

                for c in range(KC):
                    if active(g, 1, NG):
                        dve.wait_ge(f_re, 4 * (g - 1) + c + 1)
                        dve.wait_ge(f_m, 4 * (g - 1) + c + 1)
                        hm = frelu[:, 0, c, :]
                        dve.tensor_tensor(hm, hm, bank[4][:, :], ALU.mult).then_inc(f_hm, 1)
                        dve.wait_ge(f_hh, 4 * (g - 1) + c + 1)
                        low_half(dve, fhm[1][:, 0, c, :], frelu[:, 0, c, :], fhm[0][:, 0, c, :]
                                 ).then_inc(f_hl, 1)
                if active(g, 0, NG):
                    for j in range(TG):
                        cols = slice(j * P, (j + 1) * P)
                        dve.wait_ge(f_ev, 4 * g + j + 1)
                        low_half(dve, fxT[1][:, b, :, cols],
                                 bank[turned[j]][:, :].rearrange("p (c n) -> p c n", c=KC),
                                 fxT[0][:, b, :, cols]).then_inc(f_tl, 1)
                nxt = turn + (k + 1) // 4, (k + 1) % 4

                if active(g, 1, NG):
                    out_tile(0)
                pre(*nxt, 0)
                pre(*nxt, 1)
                if active(g, 1, NG):
                    out_tile(1)
                if active(g, 0, NG):
                    dve.wait_ge(f_lt, g + 1)
                    dve.tensor_copy(lg2[:, :, :].rearrange("p j e -> p (j e)"),
                                    bank[4][:, 0:2 * TG * EXP]).then_inc(f_lg, 1)
                    dve.wait_ge(f_lg, 2 * g + 1)
                    dve.tensor_tensor(lg[:, :, :], lg2[:, :, 0:EXP], lg2[:, :, EXP:], ALU.add
                                      ).then_inc(f_lg, 1)
                    need_apart(dve, f_lg, 2 * g + 2)
                    for j in range(TG):
                        ins = dve.max(mx[:, j, :], lg[:, j, :])
                    ins.then_inc(f_mx, 1)
                    dve.wait_ge(f_mx, g + 1)
                    dve.tensor_tensor(topd[:, :, 0], mx[:, :, 0], mx[:, :, 0], ALU.subtract).then_inc(f_d, 1)
                    for j in range(TG):
                        ins = dve.max_index(ix[:, j, :], mx[:, j, :], lg[:, j, :])
                    ins.then_inc(f_ix, 1)
                    dve.wait_ge(f_ix, g + 1)
                    dve.tensor_copy(ixf[:, :, 0], ix[:, :, 0]).then_inc(f_ixf, 1)
                    dve.wait_ge(f_e, g + 1)
                    dve.reciprocal(rtop[:, :, 0], tope[:, :, 0]).then_inc(f_rt, 1)
                    dve.wait_ge(f_rt, g + 1)
                    dve.tensor_tensor(gate[:, :, 0], tope[:, :, 0], rtop[:, :, 0], ALU.mult).then_inc(f_g, 1)
                    dve.wait_ge(f_g, g + 1)
                    dve.wait_ge(f_ixf, g + 1)
                    for j in range(TG):
                        ins = dve.tensor_scalar(onehot[:, j, :], iota[:, :], ixf[:, j, :],
                                                gate[:, j, :], ALU.is_equal, ALU.mult)
                    ins.then_inc(f_oh, 1)
                norm(*nxt, 0)
                norm(*nxt, 1)
                pre(*nxt, 2)
                if active(g, 1, NG):
                    out_tile(2)
                pre(*nxt, 3)
                norm(*nxt, 2)
                norm(*nxt, 3)
                if active(g, 1, NG):
                    out_tile(3)
            quad_turns(dve, ffn, 1, last=1)

        @block.tensor
        def _(pe):
            pe.wait_ge(s_wk, 16 * len(first))
            pe.wait_ge(s_bp, 16 * HEADS)
            for i in range(2 * KC):
                w = wkTs if i < KC else wqTs
                for c in range(KC):
                    last = pe.matmul(bank[i][:, c * P:(c + 1) * P], w[:, 0, c, (i % KC) * P:(i % KC + 1) * P],
                                     blockP[:, c, :], start=True, stop=True)
                last.then_inc(k_pe, 1)
            prepared(pe)
            pe.wait_ge(s_w, 16 * len(consts))

            THREE = ((0, 0), (0, 1), (1, 0))

            def product(out_, lhs, rhs, start=True, stop=True, fourth=None):
                for c in range(KC):
                    if c == KC - 1 and fourth:
                        pe.wait_ge(*fourth)
                    for i, (l, r) in enumerate(THREE):
                        last = pe.matmul(out_, lhs(l, c), rhs(r, c), start=start and c == 0 and i == 0,
                                         stop=stop and c == KC - 1 and i == 2)
                return last

            def turn_tile(psum, row):
                for c in range(KC):
                    last = pe.transpose(psum[:, c * P:(c + 1) * P], row[:, c * P:(c + 1) * P], ident[:, :])
                return last

            def keys(turn, k):
                t, b, j = 8 * turn + k, k // 4, k % 4
                if active(t, 0, NT):
                    pe.wait_ge(a_xn, t + 1)
                    need(pe, a_tl, t)
                    turn_tile(bank[5], axn[:, 0, j, :]).then_inc(a_tr, 1)
                edge_pe(pe, 0, turn, k, bank[7][:, :])
                if active(t, 3, NT):
                    turn3, kk = lagged(turn, k, 3)
                    first = isinstance(t, int) and t == 3
                    final = isinstance(t, int) and t == NT + 2
                    pe.wait_ge(a_xl, t - 2)
                    pe.wait_ge(a_pl, t - 2)
                    for c in range(KC):
                        for i, (l, r) in enumerate(THREE):
                            pe.matmul(bank[c][:, :], axr[l][:, 0, kk % 4, c * P:(c + 1) * P],
                                      aph[r][:, 0, kk % 4, :], start=first and i == 0,
                                      stop=final and i == 2, skip_group_check=True)
                    cols = slice(2, 4) if isinstance(t, int) and t - 3 >= NT - TG else slice(0, 2)
                    for n in range(2):
                        last = pe.matmul(bank[4][0:2, :], valid[:, cols],
                                         aph[n][:, 0, kk % 4, :], start=first and n == 0,
                                         stop=final and n == 1, skip_group_check=True)
                    last.then_inc(a_T, 1)
                if active(t, 0, NT):
                    pe.wait_ge(a_tl, t + 1)
                    need(pe, a_phi, t)
                    product(bank[6][:, :], lambda n, c: xT[n][:, b, c, j * P:(j + 1) * P],
                            lambda n, c: Wk[n][:, 0, c, :]).then_inc(a_kp, 1)
            turns(pe, keys, 3, last=1)

            pe.wait_ge(e_o, NT)
            pe.wait_ge(c_k2, KC + 1)
            for c in range(KC):
                last = pe.transpose(bank[5][:, 2 * c:2 * c + 2], krow[:, c * P:(c + 1) * P], ident[0:2, 0:2])
            last.then_inc(c_kr, 1)
            pe.wait_ge(c_k2, KC + 2)
            pe.wait_ge(s_fw, 32)
            for c in range(KC):
                for i in range(KC):
                    last = pe.matmul(bank[4 + c][:, 0:P], wvs[:, 0, i, c * P:(c + 1) * P],
                                     K2T[:, 0, i, c * P:(c + 1) * P], start=i == 0, stop=i == KC - 1)
                last.then_inc(c_kv, 1)
            for c in range(KC):
                pe.wait_ge(c_kvc, c + 1)
                pe.matmul(bank[c][:, :], kvT[:, c, :], wps[:, 0, c, :], start=True, stop=True
                          ).then_inc(c_m, 1)

            pe.wait_ge(c_ml, KC)
            pe.wait_ge(s_split, 4 * len(splits))

            def hidden(turn, b):
                g = 2 * turn + b
                if active(g, 0, NG):
                    for j in range(TG):
                        pe.wait_ge(b_ag, 4 * g + j + 1)
                        need(pe, b_al, 4 * (g - 1) + j + 1)
                        turn_tile(bank[means[j]], bagg[:, b, j, 0:D]).then_inc(b_tr, 1)
                if active(g, 1, NG):
                    pe.wait_ge(b_hl, 4 * g - 1)
                    for j in range(TG):
                        need(pe, b_yo, 4 * (g - 1) + j - 1)
                        product(bank[4 + j % 2][:, :], lambda n, c: bhT[n][:, 0, c, j * P:(j + 1) * P],
                                lambda n, c: W2l[n][:, 0, c, :], fourth=(b_hl, 4 * g) if j == 0 else None
                                ).then_inc(b_y, 1)
                if active(g, 0, NG):
                    pe.wait_ge(b_xt[b], 32 * (turn + 1))
                    for o in range(KC):
                        need(pe, b_th, 4 * g + o - 1)
                        ph = bank[2 + o % 2][:, :]
                        product(ph, lambda n, c: W1r[n][:, 0, c, o * P:(o + 1) * P],
                                lambda n, c: xT[n][:, b, c, :], stop=False)
                        if o == 0:
                            pe.wait_ge(b_al, 4 * (g + 1))
                        product(ph, lambda n, c: W1l[n][:, 0, c, o * P:(o + 1) * P],
                                lambda n, c: baT[n][:, 0, c, :], start=False).then_inc(b_h, 1)
            group_turns(pe, hidden, 1)

            pe.wait_ge(s_wq, 32)
            pe.wait_ge(b_th, 4 * NG)
            pe.wait_ge(b_yo, 4 * NG)

            def mix(turn, k):
                t, b, j = 8 * turn + k, k // 4, k % 4
                if active(t, 0, NT):
                    if j == 0:
                        pe.wait_ge(m_xt[b], 32 * (turn + 1))
                    need(pe, m_phi, t - 1)
                    product(bank[j % 2][:, :], lambda n, c: Wq[n][:, 0, c, j * P:(j + 1) * P],
                            lambda n, c: xT[n][:, b, c, :]).then_inc(m_q, 1)
                edge_pe(pe, 1, turn, k, bank[7][:, :])
                if active(t, 8, NT):
                    turn8, kk = lagged(turn, k, 8)
                    b8, j8 = kk // 4, kk % 4
                    if isinstance(t, int) and t == 8:
                        pe.wait_ge(s_w2r, 32)
                        pe.wait_ge(s_m, 32)
                    if j8 == 0:
                        pe.wait_ge(m_ht[b8], 32 * (turn8 + 1))
                        pe.wait_ge(m_ql, t - 8 + 4)
                    need(pe, m_po, t - 9)
                    pp, cols = bank[4 + j8 % 2][:, :], slice(j8 * P, (j8 + 1) * P)
                    product(pp, lambda n, c: mhT[n][:, b8, c, cols], lambda n, c: W2r[n][:, 0, c, :],
                            stop=False)
                    product(pp, lambda n, c: mqz[n][:, b8, c, cols], lambda n, c: M[n][:, 0, c, :],
                            start=False).then_inc(m_p, 1)
                if active(t, 2, NT):
                    j2 = (k - 2) % 4
                    pe.wait_ge(m_phi, t - 1)
                    need(pe, m_z, t - 2)
                    pe.matmul(bank[2][:, :], KS[:, j2, :], low[:, j2, :], start=True, stop=True
                              ).then_inc(m_den, 1)
            turns(pe, mix, 8, head=2)

            pe.wait_ge(s_csp, 5)

            def ffn(turn, k):
                g, b, b1_ = 4 * turn + k, k % 2, (k - 1) % 2

                def second_layer(j):
                    if not active(g, 1, NG):
                        return
                    need(pe, f_out, 4 * (g - 1) + j - 1)
                    po, cols = bank[6 + j % 2][:, :], slice(j * P, (j + 1) * P)
                    pe.matmul(po, maskT[:, b1_, cols], fb2s[:, :], start=True, stop=False)
                    if j == 0:
                        pe.wait_ge(f_hl, 4 * g - 1)
                    product(po, lambda n, c: fhm[n][:, 0, c, cols], lambda n, c: F2[n][:, 0, c, :],
                            start=False, fourth=(f_hl, 4 * g) if j == 0 else None).then_inc(f_h2, 1)

                if isinstance(g, int) and g == 1:
                    pe.wait_ge(s_f, 64)
                if active(g, 1, NG):
                    pe.wait_ge(f_tl, 4 * g)
                    for c in range(KC):
                        need(pe, f_re, 4 * (g - 1) + c - 1)
                        product(bank[2 + c % 2][:, :], lambda n, i: F1[n][:, 0, i, c * P:(c + 1) * P],
                                lambda n, i: fxT[n][:, b1_, i, :]).then_inc(f_h1, 1)
                        if c == 0:
                            pe.wait_ge(f_mtc, g)
                        need(pe, f_hm, 4 * (g - 1) + c)
                        pe.matmul(bank[4][:, :], expand[:, c, :], maskT[0:EXP, b1_, :], start=True, stop=True
                                  ).then_inc(f_m, 1)
                if active(g, 0, NG):
                    for j in range(TG):
                        pe.wait_ge(f_xn, 4 * g + j + 1)
                        if j == 3:
                            need(pe, f_re, 4 * g - 1)
                        if isinstance(g, int) and g == 0 and j == 2:
                            pe.wait_ge(m_po, NT)
                        turn_tile(bank[turned[j]], fa[:, b, j, :]).then_inc(f_tr, 1)
                second_layer(0)
                if active(g, 0, NG):
                    pe.wait_ge(f_tl, 4 * (g + 1))
                    for c in range(KC):
                        for n in range(2):
                            last = pe.matmul(bank[5][0:2 * EXP, :],
                                             wrs[:, c, :, :].rearrange("p n e -> p (n e)"),
                                             fxT[n][:, b, c, :], start=c == 0 and n == 0,
                                             stop=c == KC - 1 and n == 1)
                    last.then_inc(f_r, 1)
                second_layer(1)
                if active(g, 0, NG):
                    need_apart(pe, f_l, g + 1)
                    for j in range(TG):
                        last = pe.transpose(bank[4][:, j * 2 * EXP:(j + 1) * 2 * EXP],
                                            lgT[:, j * P:(j + 1) * P], ident[0:2 * EXP, 0:2 * EXP])
                    last.then_inc(f_lt, 1)
                second_layer(2)
                second_layer(3)
                if active(g, 0, NG):
                    need_apart(pe, f_oh, g + 1)
                    for j in range(TG):
                        last = pe.transpose(bank[5][0:STACK, j * P:(j + 1) * P], onehot[:, j, :], ident[:, :])
                    last.then_inc(f_mt, 1)
            quad_turns(pe, ffn, 1)


def kernel(x, src, dst, L0_gnn_label, L0_gnn_W1_l, L0_gnn_W1_r, L0_gnn_b1, L0_gnn_W2_l, L0_gnn_W2_r,
           L0_gnn_b2, L0_mix_w_qkv, L0_mix_proj_mat, L0_mix_w_proj, L0_mix_b_proj, L0_ffn_Wr, L0_ffn_br,
           L0_ffn_W1, L0_ffn_b1, L0_ffn_W2, L0_ffn_b2):
    import numpy as np
    import concourse.bacc as bacc
    from concourse.bass_utils import run_bass_kernel_spmd

    def lay(a):
        return np.ascontiguousarray(a)

    p = np.arange(P)
    xp = np.zeros((NP, D), np.float32)
    xp[:N] = x
    srcp = np.zeros(NP, np.int32)
    srcp[:N] = src
    dstp = (TRASH + np.arange(NP) // TG % P).astype(np.int32)
    dstp[:N] = dst
    qkv = np.asarray(L0_mix_w_qkv)
    assert NP - N <= GROUP and N % TG == 0
    arrays = {
        "x": xp, "src": srcp, "dst": dstp,
        "w1lT": lay(np.asarray(L0_gnn_W1_l).T), "w1rT": lay(np.asarray(L0_gnn_W1_r).T),
        "b1": lay(np.asarray(L0_gnn_b1).reshape(KC, P).T),
        "w2lT": lay(np.asarray(L0_gnn_W2_l).T), "w2rT": lay(np.asarray(L0_gnn_W2_r).T),
        "b2": lay(L0_gnn_b2).reshape(1, D),
        "wqT": lay(qkv[:, 0:D].T), "wkT": lay(qkv[:, D:2 * D].T), "wv": lay(qkv[:, 2 * D:3 * D]),
        "pmat": lay(L0_mix_proj_mat), "wproj": lay(L0_mix_w_proj),
        "bproj": lay(L0_mix_b_proj).reshape(1, D),
        "wr": lay(L0_ffn_Wr), "br": np.concatenate([lay(L0_ffn_br), np.zeros(EXP, np.float32)]).reshape(2 * EXP, 1),
        "f1": lay(np.asarray(L0_ffn_W1).transpose(1, 0, 2)).reshape(D, EXP * EH),
        "fb1": lay(np.asarray(L0_ffn_b1).reshape(KC, P).T),
        "f2": lay(L0_ffn_W2).reshape(EXP * EH, D), "fb2": lay(L0_ffn_b2),
        "ident_in": np.eye(P, dtype=np.float32),
        "tri_in": (p[None, :] < p[:, None]).astype(np.float32),
        "bmask_in": (p[None, :] // HD == p[:, None] // HD).astype(np.float32),
        "valid_in": np.repeat(np.stack([p >= 0, NP - GROUP + TG * p < N], axis=1), 2,
                              axis=1).astype(np.float32),
        "trash_in": (TRASH + p[:, None]).astype(np.float32),
        "expand_in": (np.arange(EXP * EH).reshape(1, KC, P) // EH
                      == np.arange(EXP)[:, None, None]).astype(np.float32),
        "iota_in": np.tile(np.where(np.arange(STACK) % LOW < EXP, np.arange(STACK) % LOW, -1
                                    ).astype(np.float32), (P, 1)),
    }
    nc = bacc.Bacc("TRN2", target_bir_lowering=False, num_devices=1)
    feeds, args = {}, {}
    for name, a in arrays.items():
        feeds["in_" + name] = a
        args[name] = nc.dram_tensor("in_" + name, a.shape, mybir.dt.from_np(a.dtype),
                                    kind="ExternalInput").ap()
    out = nc.dram_tensor("out", (NP, D), F32, kind="ExternalOutput").ap()
    build(nc, out=out, **args)
    got = run_bass_kernel_spmd(nc, [feeds], core_ids=[0])
    return got.results[0]["out"][:N]
```
